# Optimizing a Trainium2 kernel written in Bass

```python
import numpy as np
import jax
import jax.numpy as jnp

def _softmax(x, axis=-1):
    return jax.nn.softmax(x, axis=axis)

def _gelu(x):
    return jax.nn.gelu(x, approximate=True)

def _silu(x):
    return jax.nn.silu(x)

def _sigmoid(x):
    return jax.nn.sigmoid(x)

def _layernorm(x, axis=-1, eps=1e-05):
    m = jnp.mean(x, axis=axis, keepdims=True)
    v = jnp.var(x, axis=axis, keepdims=True)
    return (x - m) / jnp.sqrt(v + eps)

def _scatter_add(tgt, idx, src, axis=0):
    return tgt.at[idx].add(src)

def _segment_sum(src, seg, n):
    return jax.ops.segment_sum(src, seg, n)
kernel_name = 'mk_seq_postln_d2_jaxref_r8_00c114'

def setup_inputs(seed: int=0):
    np.random.seed(seed)
    _w = jnp.asarray

    def _L0_attn_setup():
        import jax, jax.numpy as jnp
        import numpy as np
        from jax import lax
        D_MODEL = 256
        D_STATE = 64
        D_CONV = 4
        HEADDIM = 64
        EXPAND = 2
        NGROUPS = 1
        CHUNK = 64
        D_INNER = EXPAND * D_MODEL
        NHEADS = D_INNER // HEADDIM
        CONV_DIM = D_INNER + 2 * NGROUPS * D_STATE
        D_IN_PROJ = 2 * D_INNER + 2 * NGROUPS * D_STATE + NHEADS
        BATCH, SEQ = (2, 512)
        EPS = 1e-05

        def _segsum(a):
            T = a.shape[-1]
            cs = jnp.cumsum(a, axis=-1)
            d = cs[..., :, None] - cs[..., None, :]
            mask = jnp.tril(jnp.ones((T, T), dtype=bool))
            return jnp.where(mask, d, -jnp.inf)

        def _forward(x, in_proj_w, conv_w, conv_b, dt_bias, A_log, D, norm_w, out_proj_w):
            Bsz, L, _ = x.shape
            nc = L // CHUNK
            zxbcdt = x @ in_proj_w.T
            z = zxbcdt[..., :D_INNER]
            xBC = zxbcdt[..., D_INNER:D_INNER + CONV_DIM]
            dt = zxbcdt[..., D_INNER + CONV_DIM:]
            xBC_t = jnp.transpose(xBC, (0, 2, 1))
            y = lax.conv_general_dilated(xBC_t, conv_w[:, None, :], window_strides=(1,), padding=[(D_CONV - 1, 0)], feature_group_count=CONV_DIM, dimension_numbers=('NCH', 'OIH', 'NCH'))
            y = y + conv_b[None, :, None]
            xBC = jax.nn.silu(jnp.transpose(y, (0, 2, 1)))
            xs = xBC[..., :D_INNER]
            Bm = xBC[..., D_INNER:D_INNER + NGROUPS * D_STATE]
            Cm = xBC[..., D_INNER + NGROUPS * D_STATE:]
            dt = jax.nn.softplus(dt + dt_bias)
            A = -jnp.exp(A_log)
            dA = dt * A
            xh = xs.reshape(Bsz, L, NHEADS, HEADDIM)
            Bh = jnp.repeat(Bm.reshape(Bsz, L, NGROUPS, D_STATE), NHEADS // NGROUPS, axis=2)
            Ch = jnp.repeat(Cm.reshape(Bsz, L, NGROUPS, D_STATE), NHEADS // NGROUPS, axis=2)
            xdt = xh * dt[..., None]
            Ac = dA.reshape(Bsz, nc, CHUNK, NHEADS).transpose(0, 1, 3, 2)
            A_cumsum = jnp.cumsum(Ac, axis=-1)
            Lmat = jnp.exp(_segsum(Ac))
            Cc = Ch.reshape(Bsz, nc, CHUNK, NHEADS, D_STATE)
            Bc = Bh.reshape(Bsz, nc, CHUNK, NHEADS, D_STATE)
            xc = xdt.reshape(Bsz, nc, CHUNK, NHEADS, HEADDIM)
            Y_diag = jnp.einsum('bclhn,bcshn,bchls,bcshp->bclhp', Cc, Bc, Lmat, xc)
            decay_states = jnp.exp(A_cumsum[..., -1:] - A_cumsum)
            states = jnp.einsum('bcshn,bchs,bcshp->bchpn', Bc, decay_states, xc)
            chunk_decay = jnp.exp(A_cumsum[..., -1])

            def scan_fn(h, inp):
                dec, st = inp
                prev = h
                h = dec[..., None, None] * h + st
                return (h, prev)
            h0 = jnp.zeros((Bsz, NHEADS, HEADDIM, D_STATE), x.dtype)
            _, prev_states = lax.scan(scan_fn, h0, (chunk_decay.transpose(1, 0, 2), states.transpose(1, 0, 2, 3, 4)))
            prev_states = prev_states.transpose(1, 0, 2, 3, 4)
            Y_off = jnp.einsum('bclhn,bchpn,bchl->bclhp', Cc, prev_states, jnp.exp(A_cumsum))
            Y = (Y_diag + Y_off).reshape(Bsz, L, NHEADS, HEADDIM) + D[:, None] * xh
            yf = Y.reshape(Bsz, L, D_INNER)
            yf = yf * jax.nn.silu(z)
            yf = yf * lax.rsqrt(jnp.mean(yf * yf, axis=-1, keepdims=True) + EPS) * norm_w
            return yf @ out_proj_w.T
        key = jax.random.key(seed)
        ks = jax.random.split(key, 8)
        x = jax.random.normal(ks[0], (BATCH, SEQ, D_MODEL), jnp.float32)
        in_proj_w = jax.random.normal(ks[1], (D_IN_PROJ, D_MODEL), jnp.float32) / np.sqrt(D_MODEL)
        conv_w = jax.random.normal(ks[2], (CONV_DIM, D_CONV), jnp.float32) / np.sqrt(D_CONV)
        conv_b = jnp.zeros((CONV_DIM,), jnp.float32)
        dt = jnp.exp(jax.random.uniform(ks[3], (NHEADS,)) * (np.log(0.1) - np.log(0.001)) + np.log(0.001))
        dt_bias = dt + jnp.log(-jnp.expm1(-dt))
        A_log = jnp.log(jax.random.uniform(ks[4], (NHEADS,), minval=1.0, maxval=16.0))
        D = jnp.ones((NHEADS,), jnp.float32)
        norm_w = jnp.ones((D_INNER,), jnp.float32)
        out_proj_w = jax.random.normal(ks[5], (D_MODEL, D_INNER), jnp.float32) / np.sqrt(D_INNER)
        return dict(x=x, in_proj_w=in_proj_w, conv_w=conv_w, conv_b=conv_b, dt_bias=dt_bias, A_log=A_log, D=D, norm_w=norm_w, out_proj_w=out_proj_w)
    _L0_attn_in = _L0_attn_setup()

    def _L0_ffn_setup():
        import jax, jax.numpy as jnp
        import numpy as np
        EPS = 1e-08

        def _quantize(w):
            gamma = jnp.mean(jnp.abs(w))
            return jnp.clip(jnp.round(w / (gamma + EPS)), -1.0, 1.0)

        def _bitlinear(x, w):
            return jnp.matmul(x, _quantize(w).T)
        key = jax.random.key(seed)
        k1, k2, k3, k4 = jax.random.split(key, 4)
        d, h = (256, 704)
        x = jax.random.normal(k1, (4, 256, d), dtype=jnp.float32)
        w1 = jax.random.normal(k2, (h, d), dtype=jnp.float32)
        w2 = jax.random.normal(k3, (h, d), dtype=jnp.float32)
        w3 = jax.random.normal(k4, (d, h), dtype=jnp.float32)
        return {'x': x, 'w1': w1, 'w2': w2, 'w3': w3}
    _L0_ffn_in = _L0_ffn_setup()

    def _L1_attn_setup():
        import jax, jax.numpy as jnp
        import numpy as np
        B, T, D = (2, 512, 256)
        HK, HV = (16, 32)
        AK, UV = (128, 128)
        KEY_DIM = HK * AK
        VALUE_DIM = HV * UV
        CONV_DIM = 2 * KEY_DIM + VALUE_DIM
        KCONV = 4
        CHUNK = 64
        EPS = 1e-06

        def _l2norm(x, eps=1e-06):
            return x * jax.lax.rsqrt((x * x).sum(axis=-1, keepdims=True) + eps)

        def _chunk_gated_delta_rule(q, k, v, g, beta, chunk_size=CHUNK):
            q = _l2norm(q)
            k = _l2norm(k)
            q, k, v = [x.transpose(0, 2, 1, 3).astype(jnp.float32) for x in (q, k, v)]
            beta = beta.transpose(0, 2, 1).astype(jnp.float32)
            g = g.transpose(0, 2, 1).astype(jnp.float32)
            Bs, H, Tt, A = k.shape
            U = v.shape[-1]
            pad = (chunk_size - Tt % chunk_size) % chunk_size
            if pad:
                q = jnp.pad(q, ((0, 0), (0, 0), (0, pad), (0, 0)))
                k = jnp.pad(k, ((0, 0), (0, 0), (0, pad), (0, 0)))
                v = jnp.pad(v, ((0, 0), (0, 0), (0, pad), (0, 0)))
                beta = jnp.pad(beta, ((0, 0), (0, 0), (0, pad)))
                g = jnp.pad(g, ((0, 0), (0, 0), (0, pad)))
            total = Tt + pad
            J = total // chunk_size
            q = q * A ** (-0.5)
            vb = v * beta[..., None]
            kb = k * beta[..., None]
            rs = lambda x, d: x.reshape(Bs, H, J, chunk_size, d)
            qj, kj, kbj = (rs(q, A), rs(k, A), rs(kb, A))
            vbj = rs(vb, U)
            gj = jnp.cumsum(g.reshape(Bs, H, J, chunk_size), axis=-1)
            tril = jnp.tril(jnp.ones((chunk_size, chunk_size), jnp.float32))
            decay = jnp.exp((gj[..., :, None] - gj[..., None, :]) * tril) * tril
            upper = jnp.triu(jnp.ones((chunk_size, chunk_size), bool))
            attn = -(jnp.einsum('BHJLA,BHJMA->BHJLM', kbj, kj) * decay)
            attn = jnp.where(upper, 0.0, attn)

            def correction_step(i, a):
                row = a[..., i, :]
                return a.at[..., i, :].set(row + jnp.einsum('...j,...jk->...k', row, a))
            attn = jax.lax.fori_loop(1, chunk_size, correction_step, attn)
            attn = attn + jnp.eye(chunk_size, dtype=jnp.float32)
            v_corr = jnp.einsum('BHJLM,BHJMU->BHJLU', attn, vbj)
            k_cd = jnp.einsum('BHJLM,BHJMA->BHJLA', attn, kbj * jnp.exp(gj)[..., None])
            upper1 = jnp.triu(jnp.ones((chunk_size, chunk_size), bool), k=1)

            def chunk_step(st, j):
                qc, kc = (qj[:, :, j], kj[:, :, j])
                vc, gc, kcd = (v_corr[:, :, j], gj[:, :, j], k_cd[:, :, j])
                dm = decay[:, :, j]
                intra = jnp.einsum('BHLA,BHMA->BHLM', qc, kc) * dm
                intra = jnp.where(upper1, 0.0, intra)
                v_new = vc - jnp.einsum('BHLA,BHAU->BHLU', kcd, st)
                inter = jnp.exp(gc)[..., None] * jnp.einsum('BHLA,BHAU->BHLU', qc, st)
                out_c = inter + jnp.einsum('BHLM,BHMU->BHLU', intra, v_new)
                k_dec = kc * jnp.exp(gc[:, :, -1:] - gc)[..., None]
                st = st * jnp.exp(gc[:, :, -1])[..., None, None] + jnp.einsum('BHMA,BHMU->BHAU', k_dec, v_new)
                return (st, out_c)
            st0 = jnp.zeros((Bs, H, A, U), jnp.float32)
            _, outs = jax.lax.scan(chunk_step, st0, jnp.arange(J))
            out = outs.transpose(1, 2, 0, 3, 4).reshape(Bs, H, total, U)[:, :, :Tt]
            return out.transpose(0, 2, 1, 3)

        def _forward(hidden, W_qkv, W_z, W_b, W_a, conv_weight, dt_bias, A_log, norm_w, W_out):
            Bs, Tl, _ = hidden.shape
            mixed = (hidden @ W_qkv).transpose(0, 2, 1)
            z = hidden @ W_z
            b = hidden @ W_b
            a = hidden @ W_a
            xp = jnp.pad(mixed, ((0, 0), (0, 0), (KCONV - 1, 0)))
            conv = sum((conv_weight[None, :, kk:kk + 1] * xp[:, :, kk:kk + Tl] for kk in range(KCONV)))
            mixed = jax.nn.silu(conv).transpose(0, 2, 1)
            q, k, v = jnp.split(mixed, [KEY_DIM, 2 * KEY_DIM], axis=-1)
            q = q.reshape(Bs, Tl, HK, AK)
            k = k.reshape(Bs, Tl, HK, AK)
            v = v.reshape(Bs, Tl, HV, UV)
            beta = jax.nn.sigmoid(b)
            g = -jnp.exp(A_log.astype(jnp.float32)) * jax.nn.softplus(a.astype(jnp.float32) + dt_bias)
            gqa = HV // HK
            q = jnp.repeat(q, gqa, axis=2)
            k = jnp.repeat(k, gqa, axis=2)
            core = _chunk_gated_delta_rule(q, k, v, g, beta)
            x = core.reshape(-1, UV)
            zf = z.reshape(-1, UV).astype(jnp.float32)
            xg = x * jax.nn.silu(zf)
            normed = norm_w * (xg * jax.lax.rsqrt((xg * xg).mean(-1, keepdims=True) + EPS))
            return normed.reshape(Bs, Tl, VALUE_DIM).astype(hidden.dtype) @ W_out
        key = jax.random.key(seed)
        ks = jax.random.split(key, 10)
        s = lambda d: 1.0 / np.sqrt(d)
        return {'hidden': jax.random.normal(ks[0], (B, T, D), jnp.float32), 'W_qkv': jax.random.normal(ks[1], (D, CONV_DIM), jnp.float32) * s(D), 'W_z': jax.random.normal(ks[2], (D, VALUE_DIM), jnp.float32) * s(D), 'W_b': jax.random.normal(ks[3], (D, HV), jnp.float32) * s(D), 'W_a': jax.random.normal(ks[4], (D, HV), jnp.float32) * s(D), 'conv_weight': jax.random.normal(ks[5], (CONV_DIM, KCONV), jnp.float32) * s(KCONV), 'dt_bias': jnp.ones((HV,), jnp.float32), 'A_log': jnp.log(jax.random.uniform(ks[6], (HV,), jnp.float32) * 16.0 + 0.0001), 'norm_w': jnp.ones((UV,), jnp.float32), 'W_out': jax.random.normal(ks[7], (VALUE_DIM, D), jnp.float32) * s(VALUE_DIM)}
    _L1_attn_in = _L1_attn_setup()

    def _L1_ffn_setup():
        import jax, jax.numpy as jnp
        import numpy as np
        HIDDEN = 256
        INTER = 704
        B, S = (2, 256)

        def _ternary(key, shape):
            return jax.random.randint(key, shape, -1, 2).astype(jnp.float32)
        key = jax.random.key(seed)
        ks = jax.random.split(key, 7)
        x = jax.random.normal(ks[0], (B, S, HIDDEN), dtype=jnp.float32)
        gate_w = _ternary(ks[1], (INTER, HIDDEN))
        up_w = _ternary(ks[2], (INTER, HIDDEN))
        down_w = _ternary(ks[3], (HIDDEN, INTER))
        gate_s = jax.random.uniform(ks[4], (INTER,), minval=0.01, maxval=0.1, dtype=jnp.float32)
        up_s = jax.random.uniform(ks[5], (INTER,), minval=0.01, maxval=0.1, dtype=jnp.float32)
        down_s = jax.random.uniform(ks[6], (HIDDEN,), minval=0.01, maxval=0.1, dtype=jnp.float32)
        return {'x': x, 'gate_w': gate_w, 'up_w': up_w, 'down_w': down_w, 'gate_s': gate_s, 'up_s': up_s, 'down_s': down_s}
    _L1_ffn_in = _L1_ffn_setup()
    _d = {'L0_attn_x': _L0_attn_in['x'], 'L0_attn_in_proj_w': _L0_attn_in['in_proj_w'], 'L0_attn_conv_w': _L0_attn_in['conv_w'], 'L0_attn_conv_b': _L0_attn_in['conv_b'], 'L0_attn_dt_bias': _L0_attn_in['dt_bias'], 'L0_attn_A_log': _L0_attn_in['A_log'], 'L0_attn_D': _L0_attn_in['D'], 'L0_attn_norm_w': _L0_attn_in['norm_w'], 'L0_attn_out_proj_w': _L0_attn_in['out_proj_w'], 'L0_ffn_w1': _L0_ffn_in['w1'], 'L0_ffn_w2': _L0_ffn_in['w2'], 'L0_ffn_w3': _L0_ffn_in['w3'], 'L1_attn_W_qkv': _L1_attn_in['W_qkv'], 'L1_attn_W_z': _L1_attn_in['W_z'], 'L1_attn_W_b': _L1_attn_in['W_b'], 'L1_attn_W_a': _L1_attn_in['W_a'], 'L1_attn_conv_weight': _L1_attn_in['conv_weight'], 'L1_attn_dt_bias': _L1_attn_in['dt_bias'], 'L1_attn_A_log': _L1_attn_in['A_log'], 'L1_attn_norm_w': _L1_attn_in['norm_w'], 'L1_attn_W_out': _L1_attn_in['W_out'], 'L1_ffn_gate_w': _L1_ffn_in['gate_w'], 'L1_ffn_up_w': _L1_ffn_in['up_w'], 'L1_ffn_down_w': _L1_ffn_in['down_w'], 'L1_ffn_gate_s': _L1_ffn_in['gate_s'], 'L1_ffn_up_s': _L1_ffn_in['up_s'], 'L1_ffn_down_s': _L1_ffn_in['down_s']}
    _x0 = _d['L0_attn_x']
    _d['L0_attn_x'] = jax.random.normal(jax.random.fold_in(jax.random.key(seed), 1), (2, 1024, 256), dtype=_x0.dtype)
    del _x0
    return _d

def reference(L0_attn_x, L0_attn_in_proj_w, L0_attn_conv_w, L0_attn_conv_b, L0_attn_dt_bias, L0_attn_A_log, L0_attn_D, L0_attn_norm_w, L0_attn_out_proj_w, L0_ffn_w1, L0_ffn_w2, L0_ffn_w3, L1_attn_W_qkv, L1_attn_W_z, L1_attn_W_b, L1_attn_W_a, L1_attn_conv_weight, L1_attn_dt_bias, L1_attn_A_log, L1_attn_norm_w, L1_attn_W_out, L1_ffn_gate_w, L1_ffn_up_w, L1_ffn_down_w, L1_ffn_gate_s, L1_ffn_up_s, L1_ffn_down_s):

    def _L0_attn_ref(x, in_proj_w, conv_w, conv_b, dt_bias, A_log, D, norm_w, out_proj_w):
        import jax, jax.numpy as jnp
        import numpy as np
        from jax import lax
        D_MODEL = 256
        D_STATE = 64
        D_CONV = 4
        HEADDIM = 64
        EXPAND = 2
        NGROUPS = 1
        CHUNK = 64
        D_INNER = EXPAND * D_MODEL
        NHEADS = D_INNER // HEADDIM
        CONV_DIM = D_INNER + 2 * NGROUPS * D_STATE
        D_IN_PROJ = 2 * D_INNER + 2 * NGROUPS * D_STATE + NHEADS
        BATCH, SEQ = (2, 512)
        EPS = 1e-05

        def _segsum(a):
            T = a.shape[-1]
            cs = jnp.cumsum(a, axis=-1)
            d = cs[..., :, None] - cs[..., None, :]
            mask = jnp.tril(jnp.ones((T, T), dtype=bool))
            return jnp.where(mask, d, -jnp.inf)

        def _forward(x, in_proj_w, conv_w, conv_b, dt_bias, A_log, D, norm_w, out_proj_w):
            Bsz, L, _ = x.shape
            nc = L // CHUNK
            zxbcdt = x @ in_proj_w.T
            z = zxbcdt[..., :D_INNER]
            xBC = zxbcdt[..., D_INNER:D_INNER + CONV_DIM]
            dt = zxbcdt[..., D_INNER + CONV_DIM:]
            xBC_t = jnp.transpose(xBC, (0, 2, 1))
            y = lax.conv_general_dilated(xBC_t, conv_w[:, None, :], window_strides=(1,), padding=[(D_CONV - 1, 0)], feature_group_count=CONV_DIM, dimension_numbers=('NCH', 'OIH', 'NCH'))
            y = y + conv_b[None, :, None]
            xBC = jax.nn.silu(jnp.transpose(y, (0, 2, 1)))
            xs = xBC[..., :D_INNER]
            Bm = xBC[..., D_INNER:D_INNER + NGROUPS * D_STATE]
            Cm = xBC[..., D_INNER + NGROUPS * D_STATE:]
            dt = jax.nn.softplus(dt + dt_bias)
            A = -jnp.exp(A_log)
            dA = dt * A
            xh = xs.reshape(Bsz, L, NHEADS, HEADDIM)
            Bh = jnp.repeat(Bm.reshape(Bsz, L, NGROUPS, D_STATE), NHEADS // NGROUPS, axis=2)
            Ch = jnp.repeat(Cm.reshape(Bsz, L, NGROUPS, D_STATE), NHEADS // NGROUPS, axis=2)
            xdt = xh * dt[..., None]
            Ac = dA.reshape(Bsz, nc, CHUNK, NHEADS).transpose(0, 1, 3, 2)
            A_cumsum = jnp.cumsum(Ac, axis=-1)
            Lmat = jnp.exp(_segsum(Ac))
            Cc = Ch.reshape(Bsz, nc, CHUNK, NHEADS, D_STATE)
            Bc = Bh.reshape(Bsz, nc, CHUNK, NHEADS, D_STATE)
            xc = xdt.reshape(Bsz, nc, CHUNK, NHEADS, HEADDIM)
            Y_diag = jnp.einsum('bclhn,bcshn,bchls,bcshp->bclhp', Cc, Bc, Lmat, xc)
            decay_states = jnp.exp(A_cumsum[..., -1:] - A_cumsum)
            states = jnp.einsum('bcshn,bchs,bcshp->bchpn', Bc, decay_states, xc)
            chunk_decay = jnp.exp(A_cumsum[..., -1])

            def scan_fn(h, inp):
                dec, st = inp
                prev = h
                h = dec[..., None, None] * h + st
                return (h, prev)
            h0 = jnp.zeros((Bsz, NHEADS, HEADDIM, D_STATE), x.dtype)
            _, prev_states = lax.scan(scan_fn, h0, (chunk_decay.transpose(1, 0, 2), states.transpose(1, 0, 2, 3, 4)))
            prev_states = prev_states.transpose(1, 0, 2, 3, 4)
            Y_off = jnp.einsum('bclhn,bchpn,bchl->bclhp', Cc, prev_states, jnp.exp(A_cumsum))
            Y = (Y_diag + Y_off).reshape(Bsz, L, NHEADS, HEADDIM) + D[:, None] * xh
            yf = Y.reshape(Bsz, L, D_INNER)
            yf = yf * jax.nn.silu(z)
            yf = yf * lax.rsqrt(jnp.mean(yf * yf, axis=-1, keepdims=True) + EPS) * norm_w
            return yf @ out_proj_w.T
        return _forward(x, in_proj_w, conv_w, conv_b, dt_bias, A_log, D, norm_w, out_proj_w)

    def _L0_ffn_ref(x, w1, w2, w3):
        import jax, jax.numpy as jnp
        import numpy as np
        EPS = 1e-08

        def _quantize(w):
            gamma = jnp.mean(jnp.abs(w))
            return jnp.clip(jnp.round(w / (gamma + EPS)), -1.0, 1.0)

        def _bitlinear(x, w):
            return jnp.matmul(x, _quantize(w).T)
        x1 = _bitlinear(x, w1)
        x2 = _bitlinear(x, w2)
        hidden = jax.nn.sigmoid(x1) * x2
        return _bitlinear(hidden, w3)

    def _L1_attn_ref(hidden, W_qkv, W_z, W_b, W_a, conv_weight, dt_bias, A_log, norm_w, W_out):
        import jax, jax.numpy as jnp
        import numpy as np
        B, T, D = (2, 512, 256)
        HK, HV = (16, 32)
        AK, UV = (128, 128)
        KEY_DIM = HK * AK
        VALUE_DIM = HV * UV
        CONV_DIM = 2 * KEY_DIM + VALUE_DIM
        KCONV = 4
        CHUNK = 64
        EPS = 1e-06

        def _l2norm(x, eps=1e-06):
            return x * jax.lax.rsqrt((x * x).sum(axis=-1, keepdims=True) + eps)

        def _chunk_gated_delta_rule(q, k, v, g, beta, chunk_size=CHUNK):
            q = _l2norm(q)
            k = _l2norm(k)
            q, k, v = [x.transpose(0, 2, 1, 3).astype(jnp.float32) for x in (q, k, v)]
            beta = beta.transpose(0, 2, 1).astype(jnp.float32)
            g = g.transpose(0, 2, 1).astype(jnp.float32)
            Bs, H, Tt, A = k.shape
            U = v.shape[-1]
            pad = (chunk_size - Tt % chunk_size) % chunk_size
            if pad:
                q = jnp.pad(q, ((0, 0), (0, 0), (0, pad), (0, 0)))
                k = jnp.pad(k, ((0, 0), (0, 0), (0, pad), (0, 0)))
                v = jnp.pad(v, ((0, 0), (0, 0), (0, pad), (0, 0)))
                beta = jnp.pad(beta, ((0, 0), (0, 0), (0, pad)))
                g = jnp.pad(g, ((0, 0), (0, 0), (0, pad)))
            total = Tt + pad
            J = total // chunk_size
            q = q * A ** (-0.5)
            vb = v * beta[..., None]
            kb = k * beta[..., None]
            rs = lambda x, d: x.reshape(Bs, H, J, chunk_size, d)
            qj, kj, kbj = (rs(q, A), rs(k, A), rs(kb, A))
            vbj = rs(vb, U)
            gj = jnp.cumsum(g.reshape(Bs, H, J, chunk_size), axis=-1)
            tril = jnp.tril(jnp.ones((chunk_size, chunk_size), jnp.float32))
            decay = jnp.exp((gj[..., :, None] - gj[..., None, :]) * tril) * tril
            upper = jnp.triu(jnp.ones((chunk_size, chunk_size), bool))
            attn = -(jnp.einsum('BHJLA,BHJMA->BHJLM', kbj, kj) * decay)
            attn = jnp.where(upper, 0.0, attn)

            def correction_step(i, a):
                row = a[..., i, :]
                return a.at[..., i, :].set(row + jnp.einsum('...j,...jk->...k', row, a))
            attn = jax.lax.fori_loop(1, chunk_size, correction_step, attn)
            attn = attn + jnp.eye(chunk_size, dtype=jnp.float32)
            v_corr = jnp.einsum('BHJLM,BHJMU->BHJLU', attn, vbj)
            k_cd = jnp.einsum('BHJLM,BHJMA->BHJLA', attn, kbj * jnp.exp(gj)[..., None])
            upper1 = jnp.triu(jnp.ones((chunk_size, chunk_size), bool), k=1)

            def chunk_step(st, j):
                qc, kc = (qj[:, :, j], kj[:, :, j])
                vc, gc, kcd = (v_corr[:, :, j], gj[:, :, j], k_cd[:, :, j])
                dm = decay[:, :, j]
                intra = jnp.einsum('BHLA,BHMA->BHLM', qc, kc) * dm
                intra = jnp.where(upper1, 0.0, intra)
                v_new = vc - jnp.einsum('BHLA,BHAU->BHLU', kcd, st)
                inter = jnp.exp(gc)[..., None] * jnp.einsum('BHLA,BHAU->BHLU', qc, st)
                out_c = inter + jnp.einsum('BHLM,BHMU->BHLU', intra, v_new)
                k_dec = kc * jnp.exp(gc[:, :, -1:] - gc)[..., None]
                st = st * jnp.exp(gc[:, :, -1])[..., None, None] + jnp.einsum('BHMA,BHMU->BHAU', k_dec, v_new)
                return (st, out_c)
            st0 = jnp.zeros((Bs, H, A, U), jnp.float32)
            _, outs = jax.lax.scan(chunk_step, st0, jnp.arange(J))
            out = outs.transpose(1, 2, 0, 3, 4).reshape(Bs, H, total, U)[:, :, :Tt]
            return out.transpose(0, 2, 1, 3)

        def _forward(hidden, W_qkv, W_z, W_b, W_a, conv_weight, dt_bias, A_log, norm_w, W_out):
            Bs, Tl, _ = hidden.shape
            mixed = (hidden @ W_qkv).transpose(0, 2, 1)
            z = hidden @ W_z
            b = hidden @ W_b
            a = hidden @ W_a
            xp = jnp.pad(mixed, ((0, 0), (0, 0), (KCONV - 1, 0)))
            conv = sum((conv_weight[None, :, kk:kk + 1] * xp[:, :, kk:kk + Tl] for kk in range(KCONV)))
            mixed = jax.nn.silu(conv).transpose(0, 2, 1)
            q, k, v = jnp.split(mixed, [KEY_DIM, 2 * KEY_DIM], axis=-1)
            q = q.reshape(Bs, Tl, HK, AK)
            k = k.reshape(Bs, Tl, HK, AK)
            v = v.reshape(Bs, Tl, HV, UV)
            beta = jax.nn.sigmoid(b)
            g = -jnp.exp(A_log.astype(jnp.float32)) * jax.nn.softplus(a.astype(jnp.float32) + dt_bias)
            gqa = HV // HK
            q = jnp.repeat(q, gqa, axis=2)
            k = jnp.repeat(k, gqa, axis=2)
            core = _chunk_gated_delta_rule(q, k, v, g, beta)
            x = core.reshape(-1, UV)
            zf = z.reshape(-1, UV).astype(jnp.float32)
            xg = x * jax.nn.silu(zf)
            normed = norm_w * (xg * jax.lax.rsqrt((xg * xg).mean(-1, keepdims=True) + EPS))
            return normed.reshape(Bs, Tl, VALUE_DIM).astype(hidden.dtype) @ W_out
        return _forward(hidden, W_qkv, W_z, W_b, W_a, conv_weight, dt_bias, A_log, norm_w, W_out)

    def _L1_ffn_ref(x, gate_w, up_w, down_w, gate_s, up_s, down_s):
        import jax, jax.numpy as jnp
        import numpy as np
        HIDDEN = 256
        INTER = 704
        B, S = (2, 256)

        def _ternary(key, shape):
            return jax.random.randint(key, shape, -1, 2).astype(jnp.float32)
        b, s, h = x.shape
        xf = x.reshape(b * s, h)
        g = jnp.einsum('th,ih->ti', xf, gate_w) * gate_s
        u = jnp.einsum('th,ih->ti', xf, up_w) * up_s
        hdn = jax.nn.silu(g) * u
        out = jnp.einsum('ti,hi->th', hdn, down_w) * down_s
        return out.reshape(b, s, -1)
    x = L0_attn_x
    x = _layernorm(x + _L0_attn_ref(x, L0_attn_in_proj_w, L0_attn_conv_w, L0_attn_conv_b, L0_attn_dt_bias, L0_attn_A_log, L0_attn_D, L0_attn_norm_w, L0_attn_out_proj_w), axis=-1)
    x = _layernorm(x + _L0_ffn_ref(x, L0_ffn_w1, L0_ffn_w2, L0_ffn_w3), axis=-1)
    x = _layernorm(x + _L1_attn_ref(x, L1_attn_W_qkv, L1_attn_W_z, L1_attn_W_b, L1_attn_W_a, L1_attn_conv_weight, L1_attn_dt_bias, L1_attn_A_log, L1_attn_norm_w, L1_attn_W_out), axis=-1)
    x = _layernorm(x + _L1_ffn_ref(x, L1_ffn_gate_w, L1_ffn_up_w, L1_ffn_down_w, L1_ffn_gate_s, L1_ffn_up_s, L1_ffn_down_s), axis=-1)
    return x

_drawn_inputs = setup_inputs


def setup_inputs(seed=0):
    import zlib

    import numpy as np

    out = dict(_drawn_inputs(seed))
    spreads = {'L0_attn_conv_b': (0.0, 0.1),
     'L0_attn_D': (1.0, 0.2),
     'L0_attn_norm_w': (1.0, 0.2),
     'L1_attn_dt_bias': (1.0, 0.6),
     'L1_attn_norm_w': (1.0, 0.2)}
    factors = {}
    for name, (base, spread) in spreads.items():
        noise = np.random.default_rng([zlib.crc32(name.encode()), seed]).standard_normal(out[name].shape)
        drawn = base * np.exp(spread * noise) if base else spread * noise
        out[name] = jnp.asarray(drawn.astype(out[name].dtype))
    for name, factor in factors.items():
        out[name] = (out[name] * factor).astype(out[name].dtype)
    return out
```

```python
from contextlib import ExitStack, contextmanager

import numpy as np
import concourse.bass as bass
from concourse import mybir

F32 = mybir.dt.float32
BF16 = mybir.dt.bfloat16
ALU = mybir.AluOpType
ACT = mybir.ActivationFunctionType
AX = mybir.AxisListType.X

P = 128
B, L, D = 2, 1024, 256
KT = D // P
N = B * L
W = 512
C = 128
NC = L // C
TAPS = 4
FAR = -30000.0

DI, DS, MH, HD = 512, 64, 8, 64
MIN = 2 * DI + 2 * DS + MH
FF = 704
FT = -(-FF // P)
HK, HV = 16, 32
R = HV // HK
U = NC * R
BL = 16
NBL = C // BL


class Names:
    pass


@contextmanager
def stage(nc, *names):
    with ExitStack() as ctx:
        sems = [ctx.enter_context(nc.semaphore(n)) for n in names]
        with nc.Block(no_gpsimd_drain=True) as block:
            yield (block, *sems)
        ids = [s.num for s in sems]
        nc.all_engine_barrier(sems_to_clear=range(min(ids), max(ids) + 1))


def mid(ap, n):
    p, w = ap.shape
    return ap.unsqueeze(1).to_broadcast([p, n, w])


def last(ap, n):
    p, w = ap.shape
    return ap.unsqueeze(2).to_broadcast([p, w, n])


def constants(nc, k, banks):
    with stage(nc, "zeroed", "selected", "blocks_drawn", "below_ready", "below_copied") as (
            block, zeroed, selected, blocks_drawn, below_ready, below_copied):
        @block.gpsimd
        def _(pool):
            pool.memset(k.ident[:, :], 0.0)
            pool.memset(k.identb[:, :], 0.0)
            pool.memset(k.ones[:, :], 1.0)
            pool.memset(k.mean_of[:, :], 1.0 / D)
            pool.memset(k.upto[:, :], 1.0)
            pool.memset(k.after[:, :], 1.0)
            pool.memset(k.far[:, :], 0.0)
            pool.memset(k.block_of[:, :], 1.0)
            pool.memset(k.block_after[:, :], 1.0)
            pool.memset(k.eps5[:, :], 1e-5)
            pool.memset(k.eps6[:, :], 1e-6).then_inc(zeroed, 1)
            pool.wait_ge(zeroed, 1)
            sel = pool.affine_select
            for m in (k.ident, k.identb):
                sel(out=m[:, :], in_=m[:, :], compare_op=ALU.not_equal, fill=1.0, base=0,
                    pattern=[[-1, P]], channel_multiplier=1)
            sel(out=k.upto[:, :], in_=k.upto[:, :], compare_op=ALU.is_ge, fill=0.0, base=0,
                pattern=[[1, P]], channel_multiplier=-1)
            sel(out=k.after[:, :], in_=k.after[:, :], compare_op=ALU.is_gt, fill=0.0, base=0,
                pattern=[[-1, P]], channel_multiplier=1)
            sel(out=k.far[:, :], in_=k.far[:, :], compare_op=ALU.is_ge, fill=FAR, base=0,
                pattern=[[0, 4], [1, P]], channel_multiplier=-1)
            sel(out=k.block_after[:, :], in_=k.block_after[:, :], compare_op=ALU.is_ge, fill=0.0,
                base=-BL, pattern=[[1, P]], channel_multiplier=-BL)
            sel(out=k.block_of[:, :], in_=k.block_of[:, :], compare_op=ALU.is_ge, fill=0.0,
                base=0, pattern=[[1, P]], channel_multiplier=-BL).then_inc(selected, 1)
            pool.wait_ge(selected, 1)
            sel(out=k.block_of[:, :], in_=k.block_of[:, :], compare_op=ALU.is_ge, fill=0.0,
                base=BL - 1, pattern=[[-1, P]], channel_multiplier=BL).then_inc(blocks_drawn, 1)

        @block.tensor
        def _(pe):
            pe.wait_ge(blocks_drawn, 1)
            pe.matmul(banks[0][:, 0:P], k.block_of[:, :], k.block_after[:, :], start=True,
                      stop=True).then_inc(below_ready, 1)

        @block.vector
        def _(dve):
            dve.wait_ge(below_ready, 1)
            dve.tensor_copy(k.later_block[:, :], banks[0][:, 0:P])


def layernorm(nc, k, banks, r, x, part):
    G = r.shape[2] // W
    with ExitStack() as ctx:
        sb = lambda n, s: ctx.enter_context(nc.sbuf_tensor(f"{part}_{n}", s, F32))
        d = sb("ln_d", [P, 3, KT, W])
        sq = sb("ln_sq", [P, 2, KT, W])
        std = sb("ln_std", [P, 2, W])
        inv = sb("ln_inv", [P, W])
        with stage(nc, "mean_ready", "centred", "squared", "var_ready", "std_ready", "inv_ready",
                   "written") as (block, mean_ready, centred, squared, var_ready, std_ready,
                                  inv_ready, written):
            @block.tensor
            def _(pe):
                for g in range(G + 1):
                    if g < G:
                        if g >= 2:
                            pe.wait_ge(centred, g - 1)
                        for c in range(KT):
                            mm = pe.matmul(banks[g % 2][:, :], k.mean_of[:, :],
                                           r[:, c, g * W:(g + 1) * W], start=c == 0, stop=c == KT - 1)
                        mm.then_inc(mean_ready, 1)
                    if g >= 1:
                        v = g - 1
                        pe.wait_ge(squared, v + 1)
                        if v >= 2:
                            pe.wait_ge(std_ready, v - 1)
                        for c in range(KT):
                            mm = pe.matmul(banks[2 + v % 2][:, :], k.mean_of[:, :], sq[:, v % 2, c, :],
                                           start=c == 0, stop=c == KT - 1)
                        mm.then_inc(var_ready, 1)

            @block.scalar
            def _(act):
                for g in range(G):
                    act.wait_ge(centred, g + 1)
                    if g >= 2:
                        act.wait_ge(var_ready, g - 1)
                    act.activation(sq[:, g % 2, :, :], d[:, g % 3, :, :], ACT.Square).then_inc(squared, 1)
                    act.wait_ge(var_ready, g + 1)
                    if g >= 2:
                        act.wait_ge(inv_ready, g - 1)
                    act.activation(std[:, g % 2, :], banks[2 + g % 2][:, :], ACT.Sqrt,
                                   bias=k.eps5[:, :]).then_inc(std_ready, 1)

            @block.vector
            def _(dve):
                for g in range(G + 1):
                    if g < G:
                        dve.wait_ge(mean_ready, g + 1)
                        if g >= 3:
                            dve.wait_ge(written, g - 2)
                        dve.tensor_tensor(d[:, g % 3, :, :], r[:, :, g * W:(g + 1) * W],
                                          mid(banks[g % 2][:, :], KT), ALU.subtract).then_inc(centred, 1)
                    if g >= 1:
                        v = g - 1
                        dve.wait_ge(std_ready, v + 1)
                        if v >= 1:
                            dve.wait_ge(written, v)
                        dve.reciprocal(inv[:, :], std[:, v % 2, :]).then_inc(inv_ready, 1)
                        dve.wait_ge(inv_ready, v + 1)
                        dve.tensor_tensor(x[:, :, v * W:(v + 1) * W], d[:, v % 3, :, :],
                                          mid(inv[:, :], KT), ALU.mult).then_inc(written, 1)


def ffn(nc, k, banks, x, r, part, w_up, w_gate, w_down, ternary, scales=None):
    G = N // W
    with ExitStack() as ctx:
        sb = lambda n, s: ctx.enter_context(nc.sbuf_tensor(f"{part}_{n}", s, F32))
        ws = [sb(f"ffn_w{i}", [P, KT, FT * P]) for i in range(2)]
        wd = sb("ffn_wd", [P, FT, D])
        flat = [w[:, :, :].rearrange("p k f -> p (k f)") for w in (*ws, wd)]
        h = sb("ffn_h", [P, FT, N])
        sg = sb("ffn_sg", [P, 3, W])
        gs, us, ds = (sb("ffn_gs", [P, FT]), sb("ffn_us", [P, FT]), sb("ffn_ds", [P, KT]))
        with stage(nc, "zeroed", "loaded") as (block, zeroed, loaded):
            @block.vector
            def _(dve):
                for w in ws:
                    dve.memset(w[:, :, FF:], 0.0)
                dve.memset(wd[:, FT - 1, :], 0.0).then_inc(zeroed, 1)

            @block.sync
            def _(sp):
                for w, src in zip(ws, (w_gate, w_up)):
                    sp.dma_start(w[:, :, 0:FF], src.rearrange("(k p) f -> p k f", p=P)).then_inc(loaded, 16)
                full = FF // P * P
                sp.dma_start(wd[:, 0:FT - 1, :],
                             w_down[0:full, :].rearrange("(k p) f -> p k f", p=P)).then_inc(loaded, 16)
                sp.wait_ge(zeroed, 1)
                sp.dma_start(wd[0:FF - full, FT - 1, :], w_down[full:FF, :]).then_inc(loaded, 16)
                n = 4
                if scales:
                    for dst, src in zip((gs, us, ds), scales):
                        sp.dma_start(dst[:, :], src).then_inc(loaded, 16)
                    n += 3
                sp.wait_ge(loaded, 16 * n)

        if ternary:
            size = sb("ffn_size", [P, 3])
            half = sb("ffn_half", [P, 2, 3])
            junk = sb("ffn_junk", [P, KT * FT * P])
            above = sb("ffn_above", [P, KT * FT * P])
            below = sb("ffn_below", [P, KT * FT * P])
            with stage(nc, "sized", "summed", "halved", "rounded", "compared") as (
                    block, sized, summed, halved, rounded, compared):
                @block.scalar
                def _(act):
                    for i, w in enumerate(flat):
                        act.activation(junk[:, :], w, ACT.Abs, accum_out=size[:, i:i + 1]).then_inc(sized, 1)
                        act.wait_ge(sized, i + 1)

                @block.tensor
                def _(pe):
                    pe.wait_ge(sized, 3)
                    pe.matmul(banks[0][:, 0:3], k.ones[:, :], size[:, :], start=True, stop=True)\
                      .then_inc(summed, 1)

                @block.vector
                def _(dve):
                    dve.wait_ge(summed, 1)
                    dve.tensor_scalar(half[:, 0, :], banks[0][:, 0:3], 0.5 / (FF * D), 0.5e-8,
                                      ALU.mult, ALU.add).then_inc(halved, 1)
                    dve.wait_ge(halved, 1)
                    dve.tensor_scalar(half[:, 1, :], half[:, 0, :], -1.0, None, ALU.mult).then_inc(halved, 1)
                    dve.wait_ge(halved, 2)
                    for i, w in enumerate(flat):
                        if i:
                            dve.wait_ge(rounded, i)
                        dve.tensor_scalar(above[:, :], w, half[:, 0, i:i + 1], None, ALU.is_gt)
                        dve.tensor_scalar(below[:, :], w, half[:, 1, i:i + 1], None,
                                          ALU.is_lt).then_inc(compared, 1)
                        dve.wait_ge(compared, i + 1)
                        dve.tensor_tensor(w, above[:, :], below[:, :], ALU.subtract).then_inc(rounded, 1)

        with stage(nc, "products", "gated", "hidden", "down_ready", "added") as (
                block, products, gated, hidden, down_ready, added):
            @block.tensor
            def _(pe):
                for g in range(G + 1):
                    if g < G:
                        for f in range(FT):
                            s = g * FT + f
                            if s >= 3:
                                pe.wait_ge(hidden, s - 2)
                            for i in range(2):
                                for c in range(KT):
                                    mm = pe.matmul(banks[2 * (s % 3) + i][:, :],
                                                   ws[i][:, c, f * P:(f + 1) * P],
                                                   x[:, c, g * W:(g + 1) * W], start=c == 0, stop=c == KT - 1)
                            mm.then_inc(products, 1)
                    if g >= 1:
                        v = g - 1
                        for o in range(KT):
                            if v:
                                pe.wait_ge(added, KT * (v - 1) + o + 1)
                            pe.wait_ge(hidden, FT * (v + 1))
                            for f in range(FT):
                                mm = pe.matmul(banks[6 + o][:, :], wd[:, f, o * P:(o + 1) * P],
                                               h[:, f, v * W:(v + 1) * W], start=f == 0, stop=f == FT - 1)
                            mm.then_inc(down_ready, 1)

            @block.scalar
            def _(act):
                for s in range(G * FT):
                    act.wait_ge(products, s + 1)
                    if s >= 3:
                        act.wait_ge(hidden, s - 2)
                    src = banks[2 * (s % 3)][:, :]
                    if ternary:
                        act.activation(sg[:, s % 3, :], src, ACT.Sigmoid).then_inc(gated, 1)
                    else:
                        act.activation(sg[:, s % 3, :], src, ACT.Silu,
                                       scale=gs[:, s % FT:s % FT + 1]).then_inc(gated, 1)

            @block.vector
            def _(dve):
                for g in range(G + 1):
                    if g < G:
                        for f in range(FT):
                            s = g * FT + f
                            dve.wait_ge(gated, s + 1)
                            up, out = banks[2 * (s % 3) + 1][:, :], h[:, f, g * W:(g + 1) * W]
                            if ternary:
                                dve.tensor_tensor(out, sg[:, s % 3, :], up, ALU.mult).then_inc(hidden, 1)
                            else:
                                dve.scalar_tensor_tensor(out=out, in0=up, scalar=us[:, f:f + 1],
                                                         in1=sg[:, s % 3, :], op0=ALU.mult,
                                                         op1=ALU.mult).then_inc(hidden, 1)
                    if g >= 1:
                        v = g - 1
                        for o in range(KT):
                            dve.wait_ge(down_ready, KT * v + o + 1)
                            cols = slice(v * W, (v + 1) * W)
                            if ternary:
                                dve.tensor_tensor(r[:, o, cols], x[:, o, cols], banks[6 + o][:, :],
                                                  ALU.add).then_inc(added, 1)
                            else:
                                dve.scalar_tensor_tensor(out=r[:, o, cols], in0=banks[6 + o][:, :],
                                                         scalar=ds[:, o:o + 1], in1=x[:, o, cols],
                                                         op0=ALU.mult, op1=ALU.add).then_inc(added, 1)


def projected_conv(nc, pairs, raw, steps, plain=()):
    S, T = len(steps), len(steps) + len(plain)
    with stage(nc, "product", "evacuated", "tapped", "ready", "chained") as (
            block, product, evacuated, tapped, ready, chained):
        @block.tensor
        def _(pe):
            for s, (w, cols, *_) in enumerate([*steps, *plain]):
                m = w.shape[2]
                if s >= 4:
                    pe.wait_ge(evacuated, s - 3)
                for j in range(L // W):
                    for c in range(KT):
                        mm = pe.matmul(pairs[s % 4][0:m, j * W:(j + 1) * W], w[:, c, :],
                                       cols[:, c, j * W:(j + 1) * W], start=c == 0, stop=c == KT - 1)
                mm.then_inc(product, 1)

        @block.scalar
        def _(act):
            def silu(s):
                act.wait_ge(tapped, s + 1)
                out = steps[s][4]
                act.activation(out, out, ACT.Silu).then_inc(ready, 1)

            for s, (w, cols, taps, bias, out) in enumerate(steps):
                m = w.shape[2]
                act.wait_ge(product, s + 1)
                if s >= 2:
                    act.wait_ge(tapped, s - 1)
                src = pairs[s % 4][0:m, :]
                act.activation(raw[0:m, s % 2, TAPS - 1:], src, ACT.Copy)
                if bias is None:
                    act.activation(out, src, ACT.Copy, scale=taps[:, TAPS - 1:TAPS]).then_inc(evacuated, 1)
                else:
                    act.activation(out, src, ACT.Identity, scale=taps[:, TAPS - 1:TAPS],
                                   bias=bias).then_inc(evacuated, 1)
                if s >= 1:
                    silu(s - 1)
            for s in range(S, T):
                act.wait_ge(product, s + 1)
                act.activation(plain[s - S][2], pairs[s % 4][:, :], ACT.Silu).then_inc(evacuated, 1)
                if s == S:
                    silu(S - 1)
            if S == T:
                silu(S - 1)

        @block.vector
        def _(dve):
            n = 0
            for s, (w, cols, taps, bias, out) in enumerate(steps):
                m = w.shape[2]
                dve.wait_ge(evacuated, s + 1)
                for j in range(TAPS - 1):
                    if j:
                        dve.wait_ge(chained, n)
                    ins = dve.scalar_tensor_tensor(out=out, in0=raw[0:m, s % 2, j:j + L],
                                                   scalar=taps[:, j:j + 1], in1=out,
                                                   op0=ALU.mult, op1=ALU.add)
                    if j < TAPS - 2:
                        ins.then_inc(chained, 1)
                        n += 1
                    else:
                        ins.then_inc(tapped, 1)


def mamba(nc, k, banks, pairs, x, r, a):
    with ExitStack() as ctx:
        sb = lambda n, s: ctx.enter_context(nc.sbuf_tensor(n, s, F32))
        w = sb("m_w", [P, KT, MIN])
        wo = sb("m_wo", [P, DI // P, D])
        taps = sb("m_taps", [P, 6, TAPS])
        cb = sb("m_cb", [P, 6])
        per_head = sb("m_heads", [P, 3, MH])
        nw = sb("m_nw", [P, DI // P])
        raw = sb("m_raw", [P, 2, TAPS - 1 + L])
        xbc = sb("m_xbc", [P, 6, N])
        y = sb("m_y", [P, DI // P, N])
        nega = sb("m_nega", [P, MH])
        S = sb("m_S", [DS, B, DI])
        with stage(nc, "loaded", "decayed") as (block, loaded, decayed):
            @block.sync
            def _(sp):
                sp.dma_start(w[:, :, :], a.in_proj.rearrange("(k p) f -> p k f", p=P)).then_inc(loaded, 16)
                sp.dma_start(wo[:, :, :], a.out_proj.rearrange("(k p) f -> p k f", p=P)).then_inc(loaded, 16)
                sp.dma_start(taps[:, 0:4, :], a.conv_w[0:DI, :].rearrange("(k p) j -> p k j", p=P)).then_inc(loaded, 16)
                sp.dma_start(taps[0:DS, 4:6, :], a.conv_w[DI:, :].rearrange("(k p) j -> p k j", p=DS)).then_inc(loaded, 16)
                sp.dma_start(cb[:, 0:4], a.conv_b[:, 0:4]).then_inc(loaded, 16)
                sp.dma_start(cb[0:DS, 4:6], a.conv_b[0:DS, 4:6]).then_inc(loaded, 16)
                sp.dma_start(per_head[:, :, :], a.mamba_heads).then_inc(loaded, 16)
                sp.dma_start(nw[:, :], a.mamba_norm).then_inc(loaded, 16)
                sp.wait_ge(loaded, 16 * 8)

            @block.vector
            def _(dve):
                dve.memset(raw[:, :, 0:TAPS - 1], 0.0)
                dve.memset(S[:, :, :], 0.0)
                dve.wait_ge(decayed, 1)
                dve.tensor_scalar(nega[:, :], nega[:, :], -1.0, None, ALU.mult)

            @block.scalar
            def _(act):
                act.wait_ge(loaded, 16 * 8)
                act.activation(nega[:, :], per_head[:, 1, :], ACT.Exp).then_inc(decayed, 1)

        steps = []
        for t in range(6):
            m, at = (P, DI + P * t) if t < 4 else (DS, 2 * DI + DS * (t - 4))
            for b in range(B):
                steps.append((w[:, :, at:at + m], x[:, :, b * L:(b + 1) * L], taps[0:m, t, :],
                              cb[0:m, t:t + 1], xbc[0:m, t, b * L:(b + 1) * L]))
        projected_conv(nc, pairs, raw, steps)

        with ExitStack() as inner:
            sb = lambda n, s: inner.enter_context(nc.sbuf_tensor(n, s, F32))
            xc, bx = sb("m_xc", [P, B, KT, C]), sb("m_bx", [P, B, 6, C])
            sz = sb("m_sz", [P, DI])
            dt, e, g3 = sb("m_dt", [P, 4, MH]), sb("m_e", [P, 3, MH]), sb("m_g", [P, MH])
            gU = sb("m_gU", [P, MH, C])
            G = sb("m_G", [P, MH, C])
            M = sb("m_M", [P, MH, C])
            xdt, xdd, xd, yc = (sb(n, [P, DI]) for n in ("m_xdt", "m_xdd", "m_xd", "m_yc"))
            bt = sb("m_bt", [P, DS])
            ss, sd = sb("m_ss", [P, 1]), sb("m_sd", [P, 2])
            junk = sb("m_junk", [P, DI])
            heads = lambda t: t.rearrange("p (h d) -> p h d", d=HD)
            with nc.Fori(0, NC) as i:
                with stage(nc, "staged", "z_ready", "z_gated", "dt_ready", "dt_done", "decay_ready",
                           "sums_ready", "exps_ready", "gU_ready", "spans_ready", "G_ready", "gram_ready",
                           "M_ready", "turned", "x_used", "b_turned", "b_ready", "diag_ready", "off_ready",
                           "state_ready", "S_ready", "y_ready", "squared", "std_ready", "normed",
                           "y_turned", "y_stored", "act_step", "dve_step") as (
                        block, staged, z_ready, z_gated, dt_ready, dt_done, decay_ready,
                        sums_ready, exps_ready, gU_ready, spans_ready, G_ready, gram_ready,
                        M_ready, turned, x_used, b_turned, b_ready, diag_ready, off_ready,
                        state_ready, S_ready, y_ready, squared, std_ready, normed,
                        y_turned, y_stored, act_step, dve_step):
                    @block.sync
                    def _(sp):
                        for b in range(B):
                            sp.dma_start(xc[:, b, :, :], x[:, :, bass.ds(i * C + b * L, C)]).then_inc(staged, 16)
                            sp.dma_start(bx[:, b, 0:4, :], xbc[:, 0:4, bass.ds(i * C + b * L, C)]).then_inc(staged, 16)
                            sp.dma_start(bx[0:DS, b, 4:6, :], xbc[0:DS, 4:6, bass.ds(i * C + b * L, C)]).then_inc(staged, 16)
                        sp.wait_ge(staged, 16 * 3 * B)

                    @block.tensor
                    def _(pe):
                        for b in range(B):
                            pe.wait_ge(staged, 16 * 3 * B)
                            if b:
                                pe.wait_ge(exps_ready, b)
                                pe.wait_ge(b_ready, b)
                            for c in range(KT):
                                mm = pe.matmul(banks[3][:, 0:MH], xc[:, b, c, :], w[:, c, MIN - MH:],
                                               start=c == 0, stop=c == KT - 1)
                            mm.then_inc(dt_ready, 1)
                            if b:
                                pe.wait_ge(z_gated, b)
                            for c in range(KT):
                                mm = pe.matmul(banks[0][:, :], xc[:, b, c, :], w[:, c, 0:DI],
                                               start=c == 0, stop=c == KT - 1)
                            mm.then_inc(z_ready, 1)
                            if b:
                                pe.wait_ge(y_stored, b)
                            for j in range(4):
                                mm = pe.transpose(banks[4][:, j * P:(j + 1) * P], bx[:, b, j, :], k.ident[:, :])
                            mm.then_inc(turned, 1)
                            pe.wait_ge(decay_ready, b + 1)
                            for j, m in enumerate((k.upto, k.after, k.ones)):
                                mm = pe.matmul(banks[3][:, j * MH:(j + 1) * MH], m[:, :], g3[:, :],
                                               start=True, stop=True)
                            mm.then_inc(sums_ready, 1)
                            pe.wait_ge(gU_ready, b + 1)
                            for j in range(2):
                                pe.matmul(banks[1 + j][:, :], k.after[:, :],
                                          gU[:, 4 * j:4 * j + 4, :].rearrange("p h l -> p (h l)"), start=True, stop=False)
                                mm = pe.matmul(banks[1 + j][:, :], k.identb[:, :], k.far[:, :],
                                               start=False, stop=True)
                            mm.then_inc(spans_ready, 1)
                            pe.wait_ge(exps_ready, b + 1)
                            pe.matmul(banks[3][:, 0:C], bx[0:DS, b, 4, :], bx[0:DS, b, 5, :],
                                      start=True, stop=True).then_inc(gram_ready, 1)
                            if b:
                                pe.wait_ge(y_ready, b)
                            pe.matmul(banks[6][:, :], bx[0:DS, b, 5, :], S[:, b, :], start=True,
                                      stop=True).then_inc(off_ready, 1)
                            pe.wait_ge(M_ready, b + 1)
                            pe.transpose(banks[3][:, 0:DS], bx[0:DS, b, 4, :],
                                         k.ident[0:DS, 0:DS]).then_inc(b_turned, 1)
                            pe.wait_ge(x_used, b + 1)
                            for h in range(MH):
                                mm = pe.matmul(banks[5][:, h * HD:(h + 1) * HD], M[:, h, :],
                                               xdt[:, h * HD:(h + 1) * HD], start=True, stop=True)
                            mm.then_inc(diag_ready, 1)
                            pe.wait_ge(b_ready, b + 1)
                            if b:
                                pe.wait_ge(S_ready, b)
                            pe.matmul(banks[7][0:DS, :], bt[:, :], xdd[:, :], start=True,
                                      stop=True).then_inc(state_ready, 1)
                            pe.wait_ge(normed, b + 1)
                            for j in range(4):
                                mm = pe.transpose(banks[4][:, j * P:(j + 1) * P], yc[:, j * P:(j + 1) * P],
                                                  k.ident[:, :])
                            mm.then_inc(y_turned, 1)

                    @block.scalar
                    def _(act):
                        n = 0
                        for b in range(B):
                            act.wait_ge(dt_done, 2 * b + 1)
                            act.activation(dt[:, 1, :], dt[:, 0, :], ACT.Abs).then_inc(act_step, 1)
                            act.wait_ge(act_step, n + 1)
                            act.activation(dt[:, 1, :], dt[:, 1, :], ACT.Exp, scale=-1.0).then_inc(act_step, 1)
                            act.wait_ge(act_step, n + 2)
                            act.activation(dt[:, 1, :], dt[:, 1, :], ACT.Ln, bias=k.ones[:, 0:1]).then_inc(act_step, 1)
                            n += 3
                            act.wait_ge(sums_ready, b + 1)
                            if b:
                                act.wait_ge(y_ready, b)
                                act.wait_ge(S_ready, b)
                            act.activation(e[:, :, :], banks[3][:, 0:3 * MH].rearrange("p (j h) -> p j h", h=MH),
                                           ACT.Exp).then_inc(exps_ready, 1)
                            act.wait_ge(spans_ready, b + 1)
                            act.activation(G[:, :, :].rearrange("p h l -> p (h l)"), k.psum[:, 1:3, :].rearrange("p j l -> p (j l)"), ACT.Exp)\
                               .then_inc(G_ready, 1)
                            act.wait_ge(b_turned, b + 1)
                            act.activation(bt[:, :], banks[3][:, 0:DS], ACT.Copy).then_inc(b_ready, 1)
                            act.wait_ge(z_ready, b + 1)
                            act.activation(sz[:, :], banks[0][:, :], ACT.Silu).then_inc(z_gated, 1)
                            act.wait_ge(y_ready, b + 1)
                            act.activation(junk[:, :], yc[:, :], ACT.Square, accum_out=ss[:, :]).then_inc(squared, 1)
                            act.wait_ge(squared, b + 1)
                            act.activation(sd[:, 0:1], ss[:, :], ACT.Sqrt, scale=1.0 / DI,
                                           bias=k.eps5[:, :]).then_inc(std_ready, 1)

                    @block.vector
                    def _(dve):
                        n = 0

                        def link(ins):
                            nonlocal n
                            n += 1
                            ins.then_inc(dve_step, 1)
                            dve.wait_ge(dve_step, n)

                        for b in range(B):
                            dve.wait_ge(dt_ready, b + 1)
                            link(dve.tensor_tensor(dt[:, 0, :], banks[3][:, 0:MH], per_head[:, 0, :], ALU.add))
                            dve.tensor_scalar(dt[:, 2, :], dt[:, 0, :], 0.0, None, ALU.max).then_inc(dt_done, 1)
                            dve.wait_ge(act_step, 3 * (b + 1))
                            dve.wait_ge(dt_done, 2 * b + 1)
                            dve.tensor_tensor(dt[:, 3, :], dt[:, 1, :], dt[:, 2, :], ALU.add).then_inc(dt_done, 1)
                            dve.wait_ge(dt_done, 2 * b + 2)
                            dve.tensor_tensor(g3[:, :], dt[:, 3, :], nega[:, :], ALU.mult).then_inc(decay_ready, 1)
                            dve.wait_ge(decay_ready, b + 1)
                            dve.tensor_tensor(gU[:, :, :], mid(k.upto[:, :], MH), last(g3[:, :], C),
                                              ALU.mult).then_inc(gU_ready, 1)
                            dve.wait_ge(turned, b + 1)
                            xt = heads(banks[4][:, :])
                            dve.tensor_tensor(heads(xd[:, :]), xt, last(per_head[:, 2, :], HD), ALU.mult)
                            link(dve.tensor_tensor(heads(xdt[:, :]), xt, last(dt[:, 3, :], HD), ALU.mult))
                            dve.wait_ge(exps_ready, b + 1)
                            dve.tensor_tensor(heads(xdd[:, :]), heads(xdt[:, :]), last(e[:, 1, :], HD),
                                              ALU.mult).then_inc(x_used, 1)
                            dve.wait_ge(G_ready, b + 1)
                            dve.wait_ge(gram_ready, b + 1)
                            dve.tensor_tensor(M[:, :, :], G[:, :, :], mid(banks[3][:, 0:C], MH),
                                              ALU.mult).then_inc(M_ready, 1)
                            dve.wait_ge(off_ready, b + 1)
                            link(dve.tensor_tensor(heads(yc[:, :]), heads(banks[6][:, :]), last(e[:, 0, :], HD), ALU.mult))
                            link(dve.tensor_tensor(yc[:, :], yc[:, :], xd[:, :], ALU.add))
                            dve.wait_ge(diag_ready, b + 1)
                            link(dve.tensor_tensor(yc[:, :], yc[:, :], banks[5][:, :], ALU.add))
                            dve.wait_ge(z_gated, b + 1)
                            dve.tensor_tensor(yc[:, :], yc[:, :], sz[:, :], ALU.mult).then_inc(y_ready, 1)
                            link(dve.tensor_tensor(heads(S[:, b, :]), heads(S[:, b, :]), last(e[0:DS, 2, :], HD), ALU.mult))
                            dve.wait_ge(state_ready, b + 1)
                            dve.tensor_tensor(S[:, b, :], S[:, b, :], banks[7][0:DS, :], ALU.add).then_inc(S_ready, 1)
                            dve.wait_ge(std_ready, b + 1)
                            link(dve.reciprocal(sd[:, 1:2], sd[:, 0:1]))
                            dve.tensor_scalar(yc[:, :], yc[:, :], sd[:, 1:2], None, ALU.mult).then_inc(normed, 1)
                            dve.wait_ge(y_turned, b + 1)
                            dve.tensor_tensor(y[:, :, bass.ds(i * C + b * L, C)],
                                              banks[4][:, :].rearrange("p (j l) -> p j l", l=C),
                                              last(nw[:, :], C), ALU.mult).then_inc(y_stored, 1)

        with stage(nc, "out_ready", "added") as (block, out_ready, added):
            @block.tensor
            def _(pe):
                for s in range(N // W * KT):
                    g, o = divmod(s, KT)
                    if s >= 4:
                        pe.wait_ge(added, s - 3)
                    for c in range(DI // P):
                        mm = pe.matmul(banks[s % 4][:, :], wo[:, c, o * P:(o + 1) * P],
                                       y[:, c, g * W:(g + 1) * W], start=c == 0, stop=c == DI // P - 1)
                    mm.then_inc(out_ready, 1)

            @block.vector
            def _(dve):
                for s in range(N // W * KT):
                    g, o = divmod(s, KT)
                    dve.wait_ge(out_ready, s + 1)
                    dve.tensor_tensor(r[:, o, g * W:(g + 1) * W], x[:, o, g * W:(g + 1) * W],
                                      banks[s % 4][:, :], ALU.add).then_inc(added, 1)


def delta_scalars(nc, k, banks, t, a, ctx_sb):
    HH = 2 * HV
    with stage(nc, "projected", "moved", "softened", "soft_done", "log_ready", "sums_ready", "exps_ready",
               "beta_exp", "step") as (
            block, projected, moved, softened, soft_done, log_ready, sums_ready, exps_ready, beta_exp, step):
        @block.tensor
        def _(pe):
            for c in range(NC):
                for j in range(KT):
                    mm = pe.matmul(banks[0][:, c * HH:(c + 1) * HH], t.x[:, j, c * C:(c + 1) * C],
                                   t.wba[:, j, :], start=j == 0, stop=j == KT - 1)
            mm.then_inc(projected, 1)
            pe.wait_ge(log_ready, 1)
            for j, m in enumerate((k.upto, k.after, k.ones)):
                mm = pe.matmul(banks[1 + j][:, 0:NC * HV], m[:, :],
                               t.g[:, :, :].rearrange("p c h -> p (c h)"), start=True, stop=True)
            mm.then_inc(sums_ready, 1)

        @block.vector
        def _(dve):
            ba = banks[0][:, :].rearrange("p (c h) -> p c h", h=HH)
            dve.wait_ge(projected, 1)
            dve.tensor_copy(t.beta[:, :, :], ba[:, :, 0:HV])
            dve.tensor_tensor(t.u[:, 0, :, :], ba[:, :, HV:], mid(t.heads[:, 0, :], NC), ALU.add).then_inc(moved, 1)
            dve.wait_ge(moved, 1)
            dve.tensor_scalar(t.u[:, 2, :, :], t.u[:, 0, :, :], 0.0, None, ALU.max).then_inc(step, 1)
            dve.wait_ge(softened, 3)
            dve.wait_ge(step, 1)
            dve.tensor_tensor(t.u[:, 2, :, :], t.u[:, 2, :, :], t.u[:, 1, :, :], ALU.add).then_inc(step, 1)
            dve.wait_ge(step, 2)
            dve.tensor_tensor(t.g[:, :, :], t.u[:, 2, :, :], mid(t.nega[:, :], NC), ALU.mult).then_inc(log_ready, 1)
            dve.wait_ge(beta_exp, 1)
            dve.tensor_scalar(t.beta[:, :, :], t.beta[:, :, :], 1.0, None, ALU.add).then_inc(step, 1)
            dve.wait_ge(step, 3)
            dve.reciprocal(t.beta[:, :, :], t.beta[:, :, :])

        @block.scalar
        def _(act):
            act.wait_ge(moved, 1)
            act.activation(t.beta[:, :, :], t.beta[:, :, :], ACT.Exp, scale=-1.0).then_inc(beta_exp, 1)
            act.activation(t.u[:, 1, :, :], t.u[:, 0, :, :], ACT.Abs).then_inc(softened, 1)
            act.wait_ge(softened, 1)
            act.activation(t.u[:, 1, :, :], t.u[:, 1, :, :], ACT.Exp, scale=-1.0).then_inc(softened, 1)
            act.wait_ge(softened, 2)
            act.activation(t.u[:, 1, :, :], t.u[:, 1, :, :], ACT.Ln, bias=k.ones[:, 0:1]).then_inc(softened, 1)
            act.wait_ge(sums_ready, 1)
            for j, out in enumerate((t.upto_exp, t.after_exp, t.all_exp)):
                act.activation(out[:, :, :].rearrange("p c h -> p (c h)"), banks[1 + j][:, 0:NC * HV], ACT.Exp)


BETA, UPTO, AFTER, ALL = range(4)
units = lambda m: m[:, :, :, :].rearrange("p c r l -> p (c r) l")
flat = lambda m, g: units(m)[:, 4 * g:4 * g + 4, :].rearrange("p u l -> p (u l)")
cut = lambda m, c: m[:, c * C:(c + 1) * C]
GR = U // 4
row = lambda m, h: m[bass.ds(h, 1)]


def invert(nc, k, banks, t, a, h, following):
    with stage(nc, "product", "moved", "added", "loaded", "weights_loaded") as (
            block, product, moved, added, loaded, weights_loaded):
        plan = [(t.LT, t.T, t.Z, None), (t.Z, None, t.ZT, None), (t.Z, t.TT, t.TT, t.TT),
                (t.ZT, t.Z, t.Z2, None), (t.Z2, None, t.ZT2, None), (t.Z2, t.TT, t.TT, t.TT),
                (t.ZT2, t.Z2, t.Z4, None), (t.Z4, t.TT, t.TT, t.TT), (t.eK, t.TT, t.WT, None)]
        order = [(s, g) for s in range(len(plan)) for g in range(GR)]
        mine = {True: [n for n, (s, g) in enumerate(order) if plan[s][3] is not None],
                False: [n for n, (s, g) in enumerate(order) if plan[s][3] is None]}
        place = {n: (kind, i + 1) for kind, ns in mine.items() for i, n in enumerate(ns)}

        def done(eng, n):
            kind, count = place[n]
            eng.wait_ge(added if kind else moved, count)

        @block.sync
        def _(sp):
            sp.dma_start(t.q2[:, :], t.q[:, :]).then_inc(loaded, 16)
            sp.dma_start(t.wo[:, :, :], row(a.w_out, h).rearrange("o p k f -> p (o k) f")).then_inc(weights_loaded, 16)
            if following is not None:
                load_weights(sp, t, a, following, loaded)
            sp.wait_ge(loaded, 16 + (32 if following is not None else 0))

        @block.tensor
        def _(pe):
            for n, (s, g) in enumerate(order):
                left, right, out, _ = plan[s]
                if n >= 8:
                    done(pe, n - 8)
                for m in (left, right):
                    written = [j for j in range(s) if plan[j][2] is m]
                    if written:
                        done(pe, written[-1] * GR + g)
                for u in range(4):
                    dst, lhs = banks[n % 8][:, u * C:(u + 1) * C], units(left)[:, 4 * g + u, :]
                    if right is None:
                        mm = pe.transpose(dst, lhs, t.ident[:, :])
                    else:
                        mm = pe.matmul(dst, lhs, units(right)[:, 4 * g + u, :], start=True, stop=True)
                mm.then_inc(product, 1)

        @block.scalar
        def _(act):
            for n in mine[False]:
                s, g = order[n]
                act.wait_ge(product, n + 1)
                act.activation(flat(plan[s][2], g), banks[n % 8][:, :], ACT.Copy).then_inc(moved, 1)

        @block.vector
        def _(dve):
            for n in mine[True]:
                s, g = order[n]
                dve.wait_ge(product, n + 1)
                if s > 2:
                    done(dve, [j for j in range(s) if plan[j][2] is t.TT][-1] * GR + g)
                dve.tensor_tensor(flat(plan[s][2], g), banks[n % 8][:, :], flat(plan[s][3], g),
                                  ALU.add).then_inc(added, 1)
            dve.wait_ge(weights_loaded, 16)
            wo = t.wo[:, :, :].rearrange("p r d -> p (r d)")
            dve.tensor_tensor(wo, wo, t.nw[:, :].to_broadcast([P, R * D]), ALU.mult)


def load_weights(sp, t, a, h, loaded):
    sp.dma_start(t.w[:, :, :], row(a.w_heads, h).rearrange("o p (k f) -> p (o k) f", k=KT)).then_inc(loaded, 16)
    sp.dma_start(t.taps[:, :, :], row(a.w_taps, h).rearrange("o p k f -> p (o k) f")).then_inc(loaded, 16)


def evacuate(act, t, s, src, out):
    act.activation(t.raw[:, s % 2, TAPS - 1:], src, ACT.Copy)
    return act.activation(out, src, ACT.Copy, scale=t.taps[:, s, TAPS - 1:TAPS])


def tap(dve, t, s, j, out):
    return dve.scalar_tensor_tensor(out=out, in0=t.raw[:, s % 2, j:j + L], scalar=t.taps[:, s, j:j + 1],
                                    in1=out, op0=ALU.mult, op1=ALU.add)


def scan_and_conv(nc, k, banks, t, h, scan, conv):
    pair = lambda bank: bank[:, 0:R * P]
    grouped = lambda ap: ap.rearrange("p (r l) -> p r l", r=R)
    with stage(nc, "cleared", "new_values", "values_moved", "off_ready", "off_moved", "state_add",
               "state_scaled", "state_ready", "diag_ready", "summed", "gated", "squared",
               "product", "evacuated", "chained", "tapped", "silu_done", "squares_ready", "norms_ready",
               "logd_ready") as (
            block, cleared, new_values, values_moved, off_ready, off_moved, state_add,
            state_scaled, state_ready, diag_ready, summed, gated, squared,
            product, evacuated, chained, tapped, silu_done, squares_ready, norms_ready, logd_ready):
        outs = (t.q[:, :], t.key[:, :])
        slot = (1, 0)
        conv_pair = lambda s: t.pairs[2 + s]

        @block.gpsimd
        def _(pool):
            if conv:
                pool.tensor_copy(t.logd[:, :, :], t.g[:, :, bass.ds(R * h, R)]).then_inc(logd_ready, 1)
                pool.wait_ge(logd_ready, 1)
                for c in range(NC):
                    for r in range(R):
                        pool.tensor_scalar(t.gU[:, c, r, :], k.upto[:, :], t.logd[:, c, r:r + 1], 1.0,
                                           ALU.mult, ALU.mult)

        @block.tensor
        def _(pe):
            def quarter(c, kt):
                s, j = divmod(c, 2)
                mm = pe.matmul(conv_pair(s)[:, j * W:(j + 1) * W], t.w[:, kt, s * P:(s + 1) * P],
                               t.x[:, kt, j * W:(j + 1) * W], start=kt == 0, stop=kt == KT - 1)
                if j == 1 and kt == KT - 1:
                    mm.then_inc(product, 1)

            def norms(s):
                pe.wait_ge(squares_ready, s + 1)
                for c in range(NC):
                    at = slot[s] * NC + c
                    mm = pe.matmul(banks[4][:, at:at + 1], cut(t.sq[:, slot[s], :], c), k.ones[:, 0:1],
                                   start=True, stop=True)
                mm.then_inc(norms_ready, 1)

            for c in range(NC):
                if scan:
                    if c == 0:
                        pe.wait_ge(cleared, 1)
                    else:
                        pe.wait_ge(values_moved, c)
                        pe.wait_ge(state_ready, c)
                    for r in range(R):
                        out = banks[0][:, r * P:(r + 1) * P]
                        pe.matmul(out, t.TT[:, c, r, :], t.V[:, c, r, :], start=True, stop=False)
                        mm = pe.matmul(out, t.WT[:, c, r, :], t.S[:, r, :], start=False, stop=True)
                    mm.then_inc(new_values, 1)
                    if c:
                        pe.wait_ge(off_moved, c)
                    pe.matmul(pair(banks[1]), cut(t.q2, c), t.S[:, :, :].rearrange("p r l -> p (r l)"),
                              start=True, stop=True).then_inc(off_ready, 1)
                if conv and c < 4:
                    quarter(c, 0)
                if scan:
                    pe.wait_ge(values_moved, c + 1)
                    for r in range(R):
                        mm = pe.matmul(banks[2][:, r * P:(r + 1) * P], t.Kd[:, c, r, :], t.Un[:, r, :],
                                       start=True, stop=True)
                    mm.then_inc(state_add, 1)
                    if c:
                        pe.wait_ge(gated, c)
                    for r in range(R):
                        pe.matmul(banks[3][:, r * P:(r + 1) * P], t.PT[:, c, r, :], t.Un[:, r, :],
                                  start=True, stop=True)
                    for r in range(R):
                        mm = pe.transpose(banks[3][:, (R + r) * P:(R + r + 1) * P], cut(t.z[:, r, :], c),
                                          t.ident[:, :])
                    mm.then_inc(diag_ready, 1)
                if conv and c < 4:
                    quarter(c, 1)
                if conv and c >= NC - 2:
                    norms(c - (NC - 2))

        @block.scalar
        def _(act):
            def square(c):
                act.wait_ge(gated, c + 1)
                if c:
                    act.wait_ge(squared, c)
                for r in range(R):
                    ins = act.activation(t.junk[:, r, :], t.y[:, c, r, :], ACT.Square,
                                         accum_out=t.ss[:, c * R + r:c * R + r + 1])
                ins.then_inc(squared, 1)

            def silu(s):
                act.wait_ge(tapped, s + 1)
                act.activation(outs[s], outs[s], ACT.Silu).then_inc(silu_done, 1)
                act.wait_ge(silu_done, s + 1)
                act.activation(t.sq[:, slot[s], :], outs[s], ACT.Square).then_inc(squares_ready, 1)

            for c in range(NC):
                if scan:
                    act.wait_ge(new_values, c + 1)
                    if c:
                        act.wait_ge(diag_ready, c)
                    act.activation(t.Un[:, :, :].rearrange("p r l -> p (r l)"), pair(banks[0]),
                                   ACT.Copy).then_inc(values_moved, 1)
                    act.wait_ge(off_ready, c + 1)
                    if c:
                        act.wait_ge(summed, c)
                    for r in range(R):
                        ins = act.activation(t.off[:, r, :], banks[1][:, r * P:(r + 1) * P], ACT.Copy,
                                             scale=t.mine[:, UPTO, c, r:r + 1])
                    ins.then_inc(off_moved, 1)
                if conv and c in (2, 4):
                    s = c // 2 - 1
                    act.wait_ge(product, s + 1)
                    evacuate(act, t, s, conv_pair(s), outs[s]).then_inc(evacuated, 1)
                if conv and c in (4, 6):
                    silu(c // 2 - 2)
                if scan and c >= 1:
                    square(c - 1)
            if scan:
                square(NC - 1)

        @block.vector
        def _(dve):
            n = 0
            taps_at = ((), (), ((0, 0),), ((0, 1), (0, 2)), ((1, 0),), ((1, 1), (1, 2)), (), ())
            if scan:
                dve.memset(t.S[:, :, :], 0.0).then_inc(cleared, 1)
                dve.wait_ge(cleared, 1)
            for c in range(NC):
                if scan:
                    dve.wait_ge(off_ready, c + 1)
                    dve.wait_ge(new_values, c + 1)
                    if c:
                        dve.wait_ge(state_ready, c)
                    dve.tensor_tensor(t.S[:, :, :], t.S[:, :, :], last(t.mine[:, ALL, c, :], P),
                                      ALU.mult).then_inc(state_scaled, 1)
                    dve.wait_ge(state_scaled, c + 1)
                    dve.wait_ge(state_add, c + 1)
                    dve.tensor_tensor(t.S[:, :, :], t.S[:, :, :], grouped(pair(banks[2])), ALU.add).then_inc(state_ready, 1)
                    dve.wait_ge(diag_ready, c + 1)
                    dve.wait_ge(off_moved, c + 1)
                    dve.tensor_tensor(t.y[:, c, :, :], t.off[:, :, :], grouped(pair(banks[3])), ALU.add).then_inc(summed, 1)
                    dve.wait_ge(summed, c + 1)
                    dve.scalar_tensor_tensor(out=t.y[:, c, :, :].rearrange("p r l -> p (r l)"),
                                             in0=t.y[:, c, :, :].rearrange("p r l -> p (r l)"),
                                             scalar=t.inv[:, 1, c:c + 1], in1=banks[3][:, R * P:2 * R * P],
                                             op0=ALU.mult, op1=ALU.mult).then_inc(gated, 1)
                if conv:
                    for s, j in taps_at[c]:
                        if j == 0:
                            dve.wait_ge(evacuated, s + 1)
                        else:
                            dve.wait_ge(chained, n)
                        ins = tap(dve, t, s, j, outs[s])
                        if j < TAPS - 2:
                            ins.then_inc(chained, 1)
                            n += 1
                        else:
                            ins.then_inc(tapped, 1)
            if conv:
                dve.wait_ge(norms_ready, 2)
                dve.tensor_scalar(t.norm[:, :, :], banks[4][:, 0:2 * NC].rearrange("p (s c) -> p s c", s=2), 1e-6,
                                  None, ALU.add)


def front_and_tail(nc, k, banks, t, a, h, front, tail):
    with stage(nc, "mine_ready", "roots", "spans_ready", "G_ready", "grams", "E_ready", "P_ready", "TT_cleared",
               "chain", "blocks_out", "blocks_in", "inverse_cleared", "solve_step", "solved", "back_out", "back_in",
               "product", "evacuated", "chained", "tapped", "silu_done", "K_turned", "K_read", "V_turned", "V_read",
               "std_ready", "inv_ready", "normed", "y_turned", "y_moved", "z_ready", "z_moved", "out_ready",
               "added") as (
            block, mine_ready, roots, spans_ready, G_ready, grams, E_ready, P_ready, TT_cleared,
            chain, blocks_out, blocks_in, inverse_cleared, solve_step, solved, back_out, back_in,
            product, evacuated, chained, tapped, silu_done, K_turned, K_read, V_turned, V_read,
            std_ready, inv_ready, normed, y_turned, y_moved, z_ready, z_moved, out_ready, added):
        conv_pair = lambda r: t.pairs[3 * (1 - r)]

        @block.gpsimd
        def _(pool):
            if front:
                pool.memset(t.TT[:, :, :, :], 0.0).then_inc(TT_cleared, 1)
                for c in range(NC):
                    pool.wait_ge(E_ready, c + 1)
                    pool.tensor_tensor(t.LT[:, c, :, :], t.E[:, c, :, :], mid(k.later_block[:, :], R), ALU.mult)

        @block.sync
        def _(sp):
            if front:
                sp.wait_ge(E_ready, NC)
                for r in range(NBL):
                    rows = slice(r * BL, (r + 1) * BL)
                    sp.dma_start(a.scratch[0, :, r, :, :].rearrange("u j i -> j u i"),
                                 units(t.E)[rows, :, rows]).then_inc(blocks_out, 16)
                sp.wait_ge(blocks_out, 16 * NBL)
                sp.dma_start(t.blk[:, :], a.scratch[0, :, :, :, :].rearrange("u r j i -> (u r) (j i)")).then_inc(blocks_in, 16)
                sp.wait_ge(solved, 1)
                for j in range(2):
                    sp.dma_start(a.scratch[1 + j, :, :, :, :].rearrange("u r j i -> (u r) (j i)"),
                                 t.inverse[:, j, :]).then_inc(back_out, 16)
                sp.wait_ge(back_out, 32)
                sp.wait_ge(TT_cleared, 1)
                for j, dst in enumerate((t.TT, t.T)):
                    for r in range(NBL):
                        rows = slice(r * BL, (r + 1) * BL)
                        sp.dma_start(units(dst)[rows, :, rows],
                                     a.scratch[1 + j, :, r, :, :].rearrange("u j i -> j u i")).then_inc(back_in, 16)
                sp.wait_ge(back_in, 32 * NBL)

        @block.scalar
        def _(act):
            if tail:
                act.activation(t.std[:, :], t.ss[:, :], ACT.Sqrt, scale=1.0 / P, bias=k.eps6[:, :]).then_inc(std_ready, 1)
            if front:
                act.activation(t.root[:, :, :], t.norm[:, :, :], ACT.Sqrt).then_inc(roots, 1)
                for j in range(NC // 2):
                    act.wait_ge(spans_ready, j + 1)
                    act.activation(t.G[:, 2 * j:2 * j + 2, :, :].rearrange("p c r l -> p (c r l)"), banks[j % 2][:, :],
                                   ACT.Exp).then_inc(G_ready, 1)
                for r in range(R):
                    act.wait_ge(product, r + 1)
                    evacuate(act, t, 2 + r, conv_pair(r), t.v[:, r, :]).then_inc(evacuated, 1)
                for c in range(NC):
                    act.wait_ge(K_turned, c + 1)
                    for r in range(R):
                        act.activation(t.eK[:, c, r, :], banks[2 + c % 2][:, 0:C], ACT.Copy, scale=t.sc[:, 3, c, r:r + 1])
                        ins = act.activation(t.Kd[:, c, r, :], banks[2 + c % 2][:, 0:C], ACT.Copy,
                                             scale=t.sc[:, 2, c, r:r + 1])
                    ins.then_inc(K_read, 1)
            if tail:
                for g in range(GR):
                    act.wait_ge(y_turned, g + 1)
                    act.activation(t.yT[:, :, 2 * g * C:2 * (g + 1) * C].rearrange("p r (c l) -> p c r l", l=C),
                                   banks[4 + g % 2][:, :].rearrange("p (c r l) -> p c r l", r=R, l=C),
                                   ACT.Copy).then_inc(y_moved, 1)
            if front:
                act.wait_ge(tapped, 1)
                act.activation(t.v[:, 0, :], t.v[:, 0, :], ACT.Silu).then_inc(silu_done, 1)
                for s in range(R * L // W):
                    act.wait_ge(z_ready, s + 1)
                    r, j = divmod(s, L // W)
                    act.activation(t.z[:, r, j * W:(j + 1) * W], banks[6 + s % 2][:, :], ACT.Silu).then_inc(z_moved, 1)
                act.wait_ge(tapped, 2)
                act.activation(t.v[:, 1, :], t.v[:, 1, :], ACT.Silu).then_inc(silu_done, 1)

        @block.tensor
        def _(pe):
            if front:
                for j in range(NC // 2):
                    if j >= 2:
                        pe.wait_ge(G_ready, j - 1)
                    pe.matmul(banks[j % 2][:, :], k.after[:, :],
                              t.gU[:, 2 * j:2 * j + 2, :, :].rearrange("p c r l -> p (c r l)"),
                              start=True, stop=False)
                    pe.matmul(banks[j % 2][:, :], k.identb[:, :], k.far[:, :], start=False,
                              stop=True).then_inc(spans_ready, 1)
                    for c in (2 * j, 2 * j + 1):
                        bank = banks[2 + c % 4]
                        if c >= 4:
                            pe.wait_ge(P_ready, c - 3)
                        pe.matmul(bank[:, 0:C], cut(t.key, c), cut(t.key, c), start=True, stop=True)
                        pe.matmul(bank[:, C:2 * C], cut(t.key, c), cut(t.q, c), start=True,
                                  stop=True).then_inc(grams, 1)
                for r in range(R):
                    if r:
                        pe.wait_ge(G_ready, NC // 2)
                    for j in range(L // W):
                        for kt in range(KT):
                            mm = pe.matmul(conv_pair(r)[:, j * W:(j + 1) * W], t.w[:, kt, (2 + r) * P:(3 + r) * P],
                                           t.x[:, kt, j * W:(j + 1) * W], start=kt == 0, stop=kt == KT - 1)
                    mm.then_inc(product, 1)
                pe.wait_ge(P_ready, NC)
                for c in range(NC):
                    if c >= 2:
                        pe.wait_ge(K_read, c - 1)
                    pe.transpose(banks[2 + c % 2][:, 0:C], cut(t.key, c), k.ident[:, :]).then_inc(K_turned, 1)
            if tail:
                for g in range(GR):
                    pe.wait_ge(normed, g + 1)
                    if g >= 2:
                        pe.wait_ge(y_moved, g - 1)
                    for j in range(4):
                        mm = pe.transpose(banks[4 + g % 2][:, j * C:(j + 1) * C], units(t.y)[:, 4 * g + j, :],
                                          k.ident[:, :])
                    mm.then_inc(y_turned, 1)
            if front:
                pe.wait_ge(evacuated, 1)
                for s in range(R * L // W):
                    r, j = divmod(s, L // W)
                    if s >= 2:
                        pe.wait_ge(z_moved, s - 1)
                    for kt in range(KT):
                        mm = pe.matmul(banks[6 + s % 2][:, :], t.w[:, kt, (4 + r) * P:(5 + r) * P],
                                       t.x[:, kt, j * W:(j + 1) * W], start=kt == 0, stop=kt == KT - 1)
                    mm.then_inc(z_ready, 1)
            if tail:
                if front:
                    pe.wait_ge(K_read, NC)
                pe.wait_ge(y_moved, GR)
                for s in range(KT * L // W):
                    j, o = divmod(s, KT)
                    for r in range(R):
                        mm = pe.matmul(banks[2 + s][:, :], t.wo[:, r, o * P:(o + 1) * P],
                                       t.yT[:, r, j * W:(j + 1) * W], start=r == 0, stop=r == R - 1)
                    mm.then_inc(out_ready, 1)
            if front:
                pe.wait_ge(evacuated, 2)
                pe.wait_ge(silu_done, 2)
                for c in range(NC):
                    if c >= 2:
                        pe.wait_ge(V_read, c - 1)
                    for r in range(R):
                        mm = pe.transpose(banks[c % 2][:, r * C:(r + 1) * C], cut(t.v[:, r, :], c), k.ident[:, :])
                    mm.then_inc(V_turned, 1)

        @block.vector
        def _(dve):
            n = chains = 0

            def link(ins):
                nonlocal n
                n += 1
                ins.then_inc(chain, 1)
                dve.wait_ge(chain, n)

            def taps(r):
                nonlocal chains
                dve.wait_ge(evacuated, r + 1)
                for j in range(TAPS - 1):
                    ins = tap(dve, t, 2 + r, j, t.v[:, r, :])
                    if j < TAPS - 2:
                        chains += 1
                        ins.then_inc(chained, 1)
                        dve.wait_ge(chained, chains)
                    else:
                        ins.then_inc(tapped, 1)

            if front:
                dve.reciprocal(t.inv[:, 0, :], t.norm[:, 0, :])
                for j, src in enumerate((t.beta, t.upto_exp, t.after_exp, t.all_exp)):
                    ins = dve.tensor_copy(t.mine[:, j, :, :], src[:, :, bass.ds(R * h, R)])
                ins.then_inc(mine_ready, 1)
                dve.wait_ge(mine_ready, 1)
                link(dve.tensor_tensor(t.sc[:, 0, :, :], t.mine[:, BETA, :, :], last(t.inv[:, 0, :], R), ALU.mult))
                dve.tensor_scalar(t.sc[:, 1, :, :], t.sc[:, 0, :, :], -1.0, None, ALU.mult)
                dve.tensor_tensor(t.sc[:, 2, :, :], t.sc[:, 0, :, :], t.mine[:, AFTER, :, :], ALU.mult)
                link(dve.tensor_scalar(t.sc[:, 3, :, :], t.mine[:, UPTO, :, :], -1.0, None, ALU.mult))
                for c in range(NC):
                    dve.wait_ge(grams, c + 1)
                    dve.wait_ge(G_ready, c // 2 + 1)
                    bank = banks[2 + c % 4]
                    for r in range(R):
                        ins = dve.scalar_tensor_tensor(out=t.E[:, c, r, :], in0=bank[:, 0:C],
                                                       scalar=t.sc[:, 1, c, r:r + 1], in1=t.G[:, c, r, :],
                                                       op0=ALU.mult, op1=ALU.mult)
                    ins.then_inc(E_ready, 1)
                    for r in range(R):
                        ins = dve.scalar_tensor_tensor(out=t.PT[:, c, r, :], in0=bank[:, C:2 * C],
                                                       scalar=t.sc[:, 0, c, r:r + 1], in1=t.G[:, c, r, :],
                                                       op0=ALU.mult, op1=ALU.mult)
                    ins.then_inc(P_ready, 1)
                dve.wait_ge(roots, 1)
                link(dve.reciprocal(t.inv[:, 1, :], t.root[:, 1, :]))
                dve.tensor_scalar(t.inv[:, 1, :], t.inv[:, 1, :], P ** -0.5, None, ALU.mult)
                taps(0)
            if tail:
                dve.wait_ge(std_ready, 1)
                dve.reciprocal(t.rstd[:, :], t.std[:, :]).then_inc(inv_ready, 1)
                dve.wait_ge(inv_ready, 1)
                for g in range(GR):
                    dve.tensor_tensor(units(t.y)[:, 4 * g:4 * g + 4, :], units(t.y)[:, 4 * g:4 * g + 4, :],
                                      last(t.rstd[:, 4 * g:4 * g + 4], P), ALU.mult).then_inc(normed, 1)
            if front:
                solve(dve, t, inverse_cleared, blocks_in, solve_step, solved)
                taps(1)
            if tail:
                for s in range(KT * L // W):
                    j, o = divmod(s, KT)
                    dve.wait_ge(out_ready, s + 1)
                    cols = slice(j * W, (j + 1) * W)
                    dve.tensor_tensor(t.acc[:, o, cols], t.acc[:, o, cols], banks[2 + s][:, :],
                                      ALU.add).then_inc(added, 1)
            if front:
                for c in range(NC):
                    dve.wait_ge(V_turned, c + 1)
                    dve.tensor_scalar(t.V[:, c, :, :].rearrange("p r l -> p (r l)"), banks[c % 2][:, 0:R * C],
                                      t.root[:, 0, c:c + 1], None, ALU.mult).then_inc(V_read, 1)


def solve(dve, t, cleared, blocks_in, solve_step, solved):
    tt = t.inverse[:, 0, :].rearrange("p (k i) -> p k i", i=BL)
    ebt = t.blk[:, :].rearrange("p (j i) -> p j i", i=BL)
    dve.memset(t.inverse[:, 0, :], 0.0).then_inc(cleared, 1)
    dve.wait_ge(cleared, 1)
    dve.memset(t.inverse[:, 0, ::BL + 1], 1.0).then_inc(cleared, 1)
    dve.wait_ge(cleared, 2)
    dve.wait_ge(blocks_in, 16)
    n = 0
    for i in range(1, BL):
        prod = t.prod[:, 0:i * i].rearrange("p (k j) -> p k j", j=i)
        dve.tensor_tensor(prod, tt[:, 0:i, 0:i],
                          ebt[:, 0:i, i:i + 1].rearrange("p j o -> p (o j)").unsqueeze(1).to_broadcast([P, i, i]),
                          ALU.mult).then_inc(solve_step, 1)
        n += 1
        dve.wait_ge(solve_step, n)
        dve.tensor_reduce(tt[:, 0:i, i], prod, AX, ALU.add).then_inc(solve_step, 1)
        n += 1
        dve.wait_ge(solve_step, n)
    dve.tensor_copy(t.inverse[:, 1, :].rearrange("p (i k) -> p i k", k=BL),
                    tt.rearrange("p k i -> p i k")).then_inc(solved, 1)


def delta(nc, k, banks, pairs, x, a):
    t = Names()
    with ExitStack() as ctx:
        sb = lambda n, s: ctx.enter_context(nc.sbuf_tensor("d_" + n, s, F32))
        t.x, t.acc = sb("x", [P, KT, L]), sb("acc", [P, KT, L])
        t.wba, t.heads, t.nega, t.nw = sb("wba", [P, KT, 2 * HV]), sb("heads", [P, 2, HV]), sb("nega", [P, HV]), sb("nw", [P, 1])
        t.beta, t.g, t.upto_exp, t.after_exp, t.all_exp = (
            sb(n, [P, NC, HV]) for n in ("beta", "g", "upto", "after", "all"))
        t.u = sb("u", [P, 3, NC, HV])
        t.w, t.taps, t.wo = sb("w", [P, KT, 6 * P]), sb("taps", [P, 4, TAPS]), sb("wo", [P, R, D])
        t.raw = sb("raw", [P, 2, TAPS - 1 + L])
        t.q, t.q2, t.key = sb("q", [P, L]), sb("q2", [P, L]), sb("k", [P, L])
        t.pairs, t.ident = pairs, k.ident
        t.v, t.z = sb("v", [P, R, L]), sb("z", [P, R, L])
        t.mine, t.sc, t.logd = sb("mine", [P, 4, NC, R]), sb("sc", [P, 4, NC, R]), sb("logd", [P, NC, R])
        t.norm, t.inv, t.root = (sb(n, [P, 2, NC]) for n in ("norm", "inv", "root"))
        full = lambda n: sb(n, [P, NC, R, C])
        t.E, t.G, t.LT, t.PT = full("E"), full("G"), full("LT"), full("PT")
        t.T, t.TT = full("T"), full("TT")
        t.eK, t.Kd, t.V = full("eK"), full("Kd"), full("V")
        t.ZT, t.Z2, t.ZT2 = full("ZT"), full("Z2"), full("ZT2")
        t.Z, t.Z4 = t.E, t.G
        t.WT = full("WT")
        t.blk, t.inverse, t.prod = sb("blk", [P, BL * BL]), sb("inverse", [P, 2, BL * BL]), sb("prod", [P, BL * BL])
        t.S, t.Un, t.off, t.junk = (sb(n, [P, 2, P]) for n in ("S", "Un", "off", "junk"))
        t.ss, t.std, t.rstd = (sb(n, [P, U]) for n in ("ss", "std", "rstd"))
        t.sq = t.ZT[:, :, :, :].rearrange("p c r l -> p (c r l)").rearrange("p (s l) -> p s l", s=2)
        t.gU = t.eK
        t.y, t.yT = t.Z2, t.ZT2[:, :, :, :].rearrange("p c r l -> p (c r l)").rearrange("p (r l) -> p r l", r=R)
        assert U * NBL == P
        with stage(nc, "loaded", "decayed") as (block, loaded, decayed):
            @block.sync
            def _(sp):
                sp.dma_start(t.wba[:, :, :], a.w_ba.rearrange("(k p) f -> p k f", p=P)).then_inc(loaded, 16)
                sp.dma_start(t.heads[:, :, :], a.delta_heads).then_inc(loaded, 16)
                sp.dma_start(t.nw[:, :], a.delta_norm).then_inc(loaded, 16)
                sp.wait_ge(loaded, 48)

            @block.scalar
            def _(act):
                act.wait_ge(loaded, 48)
                act.activation(t.nega[:, :], t.heads[:, 1, :], ACT.Exp).then_inc(decayed, 1)

            @block.vector
            def _(dve):
                dve.memset(t.raw[:, :, 0:TAPS - 1], 0.0)
                dve.wait_ge(decayed, 1)
                dve.tensor_scalar(t.nega[:, :], t.nega[:, :], -1.0, None, ALU.mult)

            @block.gpsimd
            def _(pool):
                pool.memset(t.T[:, :, :, :], 0.0)
        with nc.Fori(0, B) as b:
            with stage(nc, "copied") as (block, copied):
                @block.vector
                def _(dve):
                    dve.tensor_copy(t.x[:, :, :], x[:, :, bass.ds(b * L, L)]).then_inc(copied, 1)
                    dve.wait_ge(copied, 1)
                    dve.tensor_copy(t.acc[:, :, :], t.x[:, :, :])
            delta_scalars(nc, k, banks, t, a, None)
            with stage(nc, "loaded") as (block, loaded):
                @block.sync
                def _(sp):
                    load_weights(sp, t, a, 0, loaded)
                    sp.wait_ge(loaded, 32)
            scan_and_conv(nc, k, banks, t, 0, scan=False, conv=True)
            front_and_tail(nc, k, banks, t, a, 0, front=True, tail=False)
            with nc.Fori(0, HK - 1) as h:
                invert(nc, k, banks, t, a, h, h + 1)
                scan_and_conv(nc, k, banks, t, h + 1, scan=True, conv=True)
                front_and_tail(nc, k, banks, t, a, h + 1, front=True, tail=True)
            invert(nc, k, banks, t, a, HK - 1, None)
            scan_and_conv(nc, k, banks, t, None, scan=True, conv=False)
            front_and_tail(nc, k, banks, t, a, None, front=False, tail=True)
            with stage(nc, "copied") as (block, copied):
                @block.vector
                def _(dve):
                    dve.tensor_copy(x[:, :, bass.ds(b * L, L)], t.acc[:, :, :])


def program(nc, a, parts="mfdg"):
    k = Names()
    with ExitStack() as ctx:
        sb = lambda n, s, dt=F32: ctx.enter_context(nc.sbuf_tensor(n, s, dt))
        k.ident, k.identb, k.ones, k.mean_of = sb("ident", [P, P]), sb("identb", [P, P], BF16), sb("ones", [P, P]), sb("mean_of", [P, P])
        k.upto, k.after, k.later_block = sb("upto", [P, P]), sb("after", [P, P]), sb("later_block", [P, P])
        k.far = sb("far", [P, 4 * P], BF16)
        k.block_of, k.block_after = sb("block_of", [NBL, P]), sb("block_after", [NBL, P])
        k.eps5, k.eps6 = sb("eps5", [P, 1]), sb("eps6", [P, 1])
        x = sb("x", [P, KT, N])
        k.psum = ctx.enter_context(nc.psum_tensor("psum", [P, 8, W], F32))
        banks = [k.psum[:, i, :] for i in range(8)]
        pairs = [k.psum[:, 2 * i:2 * i + 2, :].rearrange("p j l -> p (j l)") for i in range(4)]
        constants(nc, k, banks)
        with stage(nc, "loaded") as (block, loaded):
            @block.sync
            def _(sp):
                sp.dma_start(x[:, :, :], a.x.rearrange("(k p) t -> p k t", p=P)).then_inc(loaded, 16)
                sp.wait_ge(loaded, 16)
        if "m" in parts:
            with nc.sbuf_tensor("r", [P, KT, N], F32) as r:
                mamba(nc, k, banks, pairs, x, r, a)
                layernorm(nc, k, banks, r, x, "mamba")
        if "f" in parts:
            with nc.sbuf_tensor("r2", [P, KT, N], F32) as r:
                ffn(nc, k, banks, x, r, "net0", a.w2, a.w1, a.w3, True)
                layernorm(nc, k, banks, r, x, "net0")
        if "d" in parts:
            delta(nc, k, banks, pairs, x, a)
            layernorm(nc, k, banks, x, x, "delta")
        if "g" in parts:
            with nc.sbuf_tensor("r3", [P, KT, N], F32) as r:
                ffn(nc, k, banks, x, r, "net1", a.up_w, a.gate_w, a.down_w, False, (a.gate_s, a.up_s, a.down_s))
                layernorm(nc, k, banks, r, x, "net1")
        with stage(nc, "stored") as (block, stored):
            @block.sync
            def _(sp):
                sp.dma_start(a.out.rearrange("(k p) t -> p k t", p=P), x[:, :, :]).then_inc(stored, 16)
                sp.wait_ge(stored, 16)


def layout(i):
    t = lambda m: np.ascontiguousarray(np.asarray(m).T)
    g = {n: np.asarray(v) for n, v in i.items()}
    rows = lambda *v: np.ascontiguousarray(np.broadcast_to(np.stack(v), (P, len(v), len(v[0]))))
    qkv, wz = g["L1_attn_W_qkv"], g["L1_attn_W_z"]
    kd = HK * P
    heads = [np.concatenate([qkv[:, h * P:(h + 1) * P], qkv[:, kd + h * P:kd + (h + 1) * P],
                             qkv[:, 2 * kd + R * h * P:2 * kd + R * (h + 1) * P],
                             wz[:, R * h * P:R * (h + 1) * P]], 1) for h in range(HK)]
    cw = g["L1_attn_conv_weight"]
    taps = [np.concatenate([cw[h * P:(h + 1) * P], cw[kd + h * P:kd + (h + 1) * P],
                            cw[2 * kd + R * h * P:2 * kd + R * (h + 1) * P]]) for h in range(HK)]
    cols = lambda v, p=P: np.ascontiguousarray(np.resize(v, (-(-len(v) // p), p)).T)
    conv_b = g["L0_attn_conv_b"]
    return {
        "x": t(g["L0_attn_x"].reshape(N, D)),
        "in_proj": t(g["L0_attn_in_proj_w"]), "out_proj": t(g["L0_attn_out_proj_w"]),
        "conv_w": g["L0_attn_conv_w"], "conv_b": np.concatenate([cols(conv_b[:DI]), np.resize(cols(conv_b[DI:], DS), (P, 2))], 1),
        "mamba_heads": rows(g["L0_attn_dt_bias"], g["L0_attn_A_log"], g["L0_attn_D"]),
        "mamba_norm": cols(g["L0_attn_norm_w"]),
        "w1": t(g["L0_ffn_w1"]), "w2": t(g["L0_ffn_w2"]), "w3": t(g["L0_ffn_w3"]),
        "w_heads": np.stack([h.reshape(KT, P, 6 * P).transpose(1, 0, 2).reshape(P, -1) for h in heads]),
        "w_taps": np.stack([h.reshape(4, P, TAPS).transpose(1, 0, 2) for h in taps]),
        "w_out": np.ascontiguousarray(g["L1_attn_W_out"].reshape(HK, R, P, D).transpose(0, 2, 1, 3)),
        "w_ba": np.concatenate([g["L1_attn_W_b"], g["L1_attn_W_a"]], 1),
        "delta_heads": rows(g["L1_attn_dt_bias"], g["L1_attn_A_log"]), "delta_norm": cols(g["L1_attn_norm_w"]),
        "gate_w": t(g["L1_ffn_gate_w"]), "up_w": t(g["L1_ffn_up_w"]), "down_w": t(g["L1_ffn_down_w"]),
        "gate_s": cols(g["L1_ffn_gate_s"]), "up_s": cols(g["L1_ffn_up_s"]), "down_s": cols(g["L1_ffn_down_s"]),
    }


def build(nc, arrays, parts="mfdg"):
    a = Names()
    dram = lambda n: nc.dram_tensor(f"in_{n}", arrays[n].shape, F32, kind="ExternalInput").ap()
    a.x, a.in_proj, a.out_proj, a.conv_w = dram("x"), dram("in_proj"), dram("out_proj"), dram("conv_w")
    a.conv_b, a.mamba_heads, a.mamba_norm = dram("conv_b"), dram("mamba_heads"), dram("mamba_norm")
    a.w1, a.w2, a.w3 = dram("w1"), dram("w2"), dram("w3")
    a.w_heads, a.w_taps, a.w_out, a.w_ba = dram("w_heads"), dram("w_taps"), dram("w_out"), dram("w_ba")
    a.delta_heads, a.delta_norm = dram("delta_heads"), dram("delta_norm")
    a.gate_w, a.up_w, a.down_w, a.gate_s = dram("gate_w"), dram("up_w"), dram("down_w"), dram("gate_s")
    a.up_s, a.down_s = dram("up_s"), dram("down_s")
    a.scratch = nc.dram_tensor("scratch", (3, U, NBL, BL, BL), F32, kind="Internal").ap()
    a.out = nc.dram_tensor("out", (D, N), F32, kind="ExternalOutput").ap()
    program(nc, a, parts)


def kernel(**inputs):
    import concourse.bacc as bacc
    from concourse.bass_utils import run_bass_kernel_spmd

    arrays = {n: np.ascontiguousarray(v) for n, v in layout(inputs).items()}
    nc = bacc.Bacc("TRN2", target_bir_lowering=False, num_devices=1)
    build(nc, arrays)
    result = run_bass_kernel_spmd(nc, [{f"in_{n}": v for n, v in arrays.items()}], core_ids=[0])
    return np.ascontiguousarray(result.results[0]["out"].T).reshape(B, L, D)
```

```python
from contextlib import ExitStack, contextmanager

import numpy as np
import concourse.bass as bass
from concourse import mybir

F32 = mybir.dt.float32
BF16 = mybir.dt.bfloat16
F32R = mybir.dt.float32r
ALU = mybir.AluOpType
ACT = mybir.ActivationFunctionType
AX = mybir.AxisListType.X

P = 128
B, L, D = 2, 1024, 256
KT = D // P
N = B * L
W = 512
C = 128
NC = L // C
TAPS = 4
FAR = -30000.0

DI, DS, MH, HD = 512, 64, 8, 64
MIN = 2 * DI + 2 * DS + MH
FF = 704
FT = -(-FF // P)
HK, HV = 16, 32
R = HV // HK
U = NC * R
BL = 16
NBL = C // BL


class Names:
    pass


@contextmanager
def stage(nc, *names):
    with ExitStack() as ctx:
        sems = [ctx.enter_context(nc.semaphore(n)) for n in names]
        with nc.Block(no_gpsimd_drain=True) as block:
            yield (block, *sems)
        ids = [s.num for s in sems]
        nc.all_engine_barrier(sems_to_clear=range(min(ids), max(ids) + 1))


def mid(ap, n):
    p, w = ap.shape
    return ap.unsqueeze(1).to_broadcast([p, n, w])


def last(ap, n):
    p, w = ap.shape
    return ap.unsqueeze(2).to_broadcast([p, w, n])


def constants(nc, k, banks):
    with stage(nc, "zeroed", "selected", "blocks_drawn", "below_ready", "below_copied") as (
            block, zeroed, selected, blocks_drawn, below_ready, below_copied):
        @block.gpsimd
        def _(pool):
            pool.memset(k.ident[:, :], 0.0)
            pool.memset(k.identb[:, :], 0.0)
            pool.memset(k.ones[:, :], 1.0)
            pool.memset(k.mean_of[:, :], 1.0 / D)
            pool.memset(k.upto[:, :], 1.0)
            pool.memset(k.after[:, :], 1.0)
            pool.memset(k.far[:, :], 0.0)
            pool.memset(k.block_of[:, :], 1.0)
            pool.memset(k.block_after[:, :], 1.0)
            pool.memset(k.eps5[:, :], 1e-5)
            pool.memset(k.eps6[:, :], 1e-6).then_inc(zeroed, 1)
            pool.wait_ge(zeroed, 1)
            sel = pool.affine_select
            for m in (k.ident, k.identb):
                sel(out=m[:, :], in_=m[:, :], compare_op=ALU.not_equal, fill=1.0, base=0,
                    pattern=[[-1, P]], channel_multiplier=1)
            sel(out=k.upto[:, :], in_=k.upto[:, :], compare_op=ALU.is_ge, fill=0.0, base=0,
                pattern=[[1, P]], channel_multiplier=-1)
            sel(out=k.after[:, :], in_=k.after[:, :], compare_op=ALU.is_gt, fill=0.0, base=0,
                pattern=[[-1, P]], channel_multiplier=1)
            sel(out=k.far[:, :], in_=k.far[:, :], compare_op=ALU.is_ge, fill=FAR, base=0,
                pattern=[[0, 4], [1, P]], channel_multiplier=-1)
            sel(out=k.block_after[:, :], in_=k.block_after[:, :], compare_op=ALU.is_ge, fill=0.0,
                base=-BL, pattern=[[1, P]], channel_multiplier=-BL)
            sel(out=k.block_of[:, :], in_=k.block_of[:, :], compare_op=ALU.is_ge, fill=0.0,
                base=0, pattern=[[1, P]], channel_multiplier=-BL).then_inc(selected, 1)
            pool.wait_ge(selected, 1)
            sel(out=k.block_of[:, :], in_=k.block_of[:, :], compare_op=ALU.is_ge, fill=0.0,
                base=BL - 1, pattern=[[-1, P]], channel_multiplier=BL).then_inc(blocks_drawn, 1)

        @block.tensor
        def _(pe):
            pe.wait_ge(blocks_drawn, 1)
            pe.matmul(banks[0][:, 0:P], k.block_of[:, :], k.block_after[:, :], start=True,
                      stop=True).then_inc(below_ready, 1)

        @block.vector
        def _(dve):
            dve.wait_ge(below_ready, 1)
            dve.tensor_copy(k.later_block[:, :], banks[0][:, 0:P])
            dve.tensor_copy(k.after_r[:, :], k.after[:, :])


def layernorm(nc, k, banks, r, x, part):
    G = r.shape[2] // W
    with ExitStack() as ctx:
        sb = lambda n, s: ctx.enter_context(nc.sbuf_tensor(f"{part}_{n}", s, F32))
        d = sb("ln_d", [P, 3, KT, W])
        sq = sb("ln_sq", [P, 2, KT, W])
        std = sb("ln_std", [P, 2, W])
        inv = sb("ln_inv", [P, W])
        with stage(nc, "mean_ready", "centred", "squared", "var_ready", "std_ready", "inv_ready",
                   "written") as (block, mean_ready, centred, squared, var_ready, std_ready,
                                  inv_ready, written):
            @block.tensor
            def _(pe):
                for g in range(G + 1):
                    if g < G:
                        if g >= 2:
                            pe.wait_ge(centred, g - 1)
                        for c in range(KT):
                            mm = pe.matmul(banks[g % 2][:, :], k.mean_of[:, :],
                                           r[:, c, g * W:(g + 1) * W], start=c == 0, stop=c == KT - 1)
                        mm.then_inc(mean_ready, 1)
                    if g >= 1:
                        v = g - 1
                        pe.wait_ge(squared, v + 1)
                        if v >= 2:
                            pe.wait_ge(std_ready, v - 1)
                        for c in range(KT):
                            mm = pe.matmul(banks[2 + v % 2][:, :], k.mean_of[:, :], sq[:, v % 2, c, :],
                                           start=c == 0, stop=c == KT - 1)
                        mm.then_inc(var_ready, 1)

            @block.scalar
            def _(act):
                for g in range(G):
                    act.wait_ge(centred, g + 1)
                    if g >= 2:
                        act.wait_ge(var_ready, g - 1)
                    act.activation(sq[:, g % 2, :, :], d[:, g % 3, :, :], ACT.Square).then_inc(squared, 1)
                    act.wait_ge(var_ready, g + 1)
                    if g >= 2:
                        act.wait_ge(inv_ready, g - 1)
                    act.activation(std[:, g % 2, :], banks[2 + g % 2][:, :], ACT.Sqrt,
                                   bias=k.eps5[:, :]).then_inc(std_ready, 1)

            @block.vector
            def _(dve):
                for g in range(G + 1):
                    if g < G:
                        dve.wait_ge(mean_ready, g + 1)
                        if g >= 3:
                            dve.wait_ge(written, g - 2)
                        dve.tensor_tensor(d[:, g % 3, :, :], r[:, :, g * W:(g + 1) * W],
                                          mid(banks[g % 2][:, :], KT), ALU.subtract).then_inc(centred, 1)
                    if g >= 1:
                        v = g - 1
                        dve.wait_ge(std_ready, v + 1)
                        if v >= 1:
                            dve.wait_ge(written, v)
                        dve.reciprocal(inv[:, :], std[:, v % 2, :]).then_inc(inv_ready, 1)
                        dve.wait_ge(inv_ready, v + 1)
                        dve.tensor_tensor(x[:, :, v * W:(v + 1) * W], d[:, v % 3, :, :],
                                          mid(inv[:, :], KT), ALU.mult).then_inc(written, 1)


def ffn(nc, k, banks, x, r, part, w_up, w_gate, w_down, ternary, scales=None):
    G = N // W
    with ExitStack() as ctx:
        sb = lambda n, s, dt=F32: ctx.enter_context(nc.sbuf_tensor(f"{part}_{n}", s, dt))
        sizes = ([P, KT, FT * P], [P, KT, FT * P], [P, FT, D])
        whole = [sb(f"ffn_w{i}", s) for i, s in enumerate(sizes)]
        flat = lambda m: m[:, :, :].rearrange("p k f -> p (k f)")
        h = sb("ffn_h", [P, 4, W] if ternary else [P, 2, FT, W])
        if ternary:
            weights = [sb(f"ffn_wt{i}", s, F32R) for i, s in enumerate(sizes)]
            xs = sb("ffn_xs", [P, 2, 2, KT, W], F32R)
            hs = sb("ffn_hs", [P, 2, 2, FT, W], F32R)
        else:
            weights = whole
        parts = 2 if ternary else 1
        x_part = lambda g, n, c: xs[:, g % 2, n, c, :] if ternary else x[:, c, g * W:(g + 1) * W]
        h_part = lambda g, n, f: hs[:, g % 2, n, f, :] if ternary else h[:, g % 2, f, :]
        sg = sb("ffn_sg", [P, 3, W])
        gs, us, ds = (sb("ffn_gs", [P, FT]), sb("ffn_us", [P, FT]), sb("ffn_ds", [P, KT]))
        with stage(nc, "zeroed", "loaded") as (block, zeroed, loaded):
            @block.vector
            def _(dve):
                for w in whole[0:2]:
                    dve.memset(w[:, :, FF:], 0.0)
                dve.memset(whole[2][:, FT - 1, :], 0.0).then_inc(zeroed, 1)

            @block.sync
            def _(sp):
                for w, src in zip(whole, (w_gate, w_up)):
                    sp.dma_start(w[:, :, 0:FF], src.rearrange("(k p) f -> p k f", p=P)).then_inc(loaded, 16)
                full = FF // P * P
                wd = whole[2]
                sp.dma_start(wd[:, 0:FT - 1, :],
                             w_down[0:full, :].rearrange("(k p) f -> p k f", p=P)).then_inc(loaded, 16)
                sp.wait_ge(zeroed, 1)
                sp.dma_start(wd[0:FF - full, FT - 1, :], w_down[full:FF, :]).then_inc(loaded, 16)
                n = 4
                if scales:
                    for dst, src in zip((gs, us, ds), scales):
                        sp.dma_start(dst[:, :], src).then_inc(loaded, 16)
                    n += 3
                sp.wait_ge(loaded, 16 * n)

        if ternary:
            size = sb("ffn_size", [P, 3])
            half = sb("ffn_half", [P, 2, 3])
            above = sb("ffn_above", [P, KT * FT * P])
            below = sb("ffn_below", [P, KT * FT * P])
            with stage(nc, "sized", "summed", "halved", "rounded", "compared") as (
                    block, sized, summed, halved, rounded, compared):
                @block.scalar
                def _(act):
                    for i, w in enumerate(whole):
                        act.activation(above[:, :], flat(w), ACT.Abs, accum_out=size[:, i:i + 1]).then_inc(sized, 1)
                        act.wait_ge(sized, i + 1)

                @block.tensor
                def _(pe):
                    pe.wait_ge(sized, 3)
                    pe.matmul(banks[0][:, 0:3], k.ones[:, :], size[:, :], start=True, stop=True)\
                      .then_inc(summed, 1)

                @block.vector
                def _(dve):
                    dve.wait_ge(summed, 1)
                    dve.tensor_scalar(half[:, 0, :], banks[0][:, 0:3], 0.5 / (FF * D), 0.5e-8,
                                      ALU.mult, ALU.add).then_inc(halved, 1)
                    dve.wait_ge(halved, 1)
                    dve.tensor_scalar(half[:, 1, :], half[:, 0, :], -1.0, None, ALU.mult).then_inc(halved, 1)
                    dve.wait_ge(halved, 2)
                    for i, w in enumerate(whole):
                        if i:
                            dve.wait_ge(rounded, i)
                        dve.tensor_scalar(above[:, :], flat(w), half[:, 0, i:i + 1], None, ALU.is_gt)
                        dve.tensor_scalar(below[:, :], flat(w), half[:, 1, i:i + 1], None,
                                          ALU.is_lt).then_inc(compared, 1)
                        dve.wait_ge(compared, i + 1)
                        dve.tensor_tensor(flat(weights[i]), above[:, :], below[:, :], ALU.subtract).then_inc(rounded, 1)

        with stage(nc, "x_high", "x_split", "products", "gated", "hidden", "h_high", "h_split", "down_ready",
                   "added") as (block, x_high, x_split, products, gated, hidden, h_high, h_split, down_ready, added):
            cols = lambda g: slice(g * W, (g + 1) * W)

            @block.tensor
            def _(pe):
                for g in range(G + 1):
                    if g < G:
                        if ternary:
                            pe.wait_ge(x_split, g + 1)
                        for f in range(FT):
                            s = g * FT + f
                            if s >= 3:
                                pe.wait_ge(hidden, s - 2)
                            for i in range(2):
                                for c in range(KT):
                                    for n in range(parts):
                                        mm = pe.matmul(banks[2 * (s % 3) + i][:, :],
                                                       weights[i][:, c, f * P:(f + 1) * P], x_part(g, n, c),
                                                       start=c == 0 and n == 0, stop=c == KT - 1 and n == parts - 1)
                            mm.then_inc(products, 1)
                    if g >= 1:
                        v = g - 1
                        for o in range(KT):
                            if v:
                                pe.wait_ge(added, KT * (v - 1) + o + 1)
                            pe.wait_ge(h_split if ternary else hidden, FT * (v + 1))
                            for f in range(FT):
                                for n in range(parts):
                                    mm = pe.matmul(banks[6 + o][:, :], weights[2][:, f, o * P:(o + 1) * P],
                                                   h_part(v, n, f), start=f == 0 and n == 0,
                                                   stop=f == FT - 1 and n == parts - 1)
                            mm.then_inc(down_ready, 1)

            @block.scalar
            def _(act):
                def take_x(g):
                    if g >= 2:
                        act.wait_ge(products, FT * (g - 1))
                    act.activation(xs[:, g % 2, 0, :, :], x[:, :, cols(g)], ACT.Copy).then_inc(x_high, 1)

                def take_h(s):
                    g, f = divmod(s, FT)
                    act.wait_ge(hidden, s + 1)
                    if g >= 2 and f == 0:
                        act.wait_ge(down_ready, KT * (g - 1))
                    act.activation(hs[:, g % 2, 0, f, :], h[:, s % 4, :], ACT.Copy).then_inc(h_high, 1)

                if ternary:
                    take_x(0)
                for s in range(G * FT):
                    g, f = divmod(s, FT)
                    act.wait_ge(products, s + 1)
                    if s >= 3:
                        act.wait_ge(hidden, s - 2)
                    src = banks[2 * (s % 3)][:, :]
                    if ternary:
                        act.activation(sg[:, s % 3, :], src, ACT.Sigmoid).then_inc(gated, 1)
                    else:
                        act.activation(sg[:, s % 3, :], src, ACT.Silu, scale=gs[:, f:f + 1]).then_inc(gated, 1)
                    if ternary and s:
                        take_h(s - 1)
                    if ternary and f == 1 and g + 1 < G:
                        take_x(g + 1)
                if ternary:
                    take_h(G * FT - 1)

            @block.gpsimd
            def _(pool):
                for s in range(G * FT if ternary else 0):
                    g, f = divmod(s, FT)
                    pool.wait_ge(h_high, s + 1)
                    if g >= 2 and f == 0:
                        pool.wait_ge(down_ready, KT * (g - 1))
                    pool.tensor_tensor(hs[:, g % 2, 1, f, :], h[:, s % 4, :], hs[:, g % 2, 0, f, :].bitcast(F32),
                                       ALU.subtract).then_inc(h_split, 1)

            @block.vector
            def _(dve):
                def split_x(g):
                    dve.wait_ge(x_high, g + 1)
                    dve.tensor_tensor(xs[:, g % 2, 1, :, :], x[:, :, cols(g)], xs[:, g % 2, 0, :, :].bitcast(F32),
                                      ALU.subtract).then_inc(x_split, 1)

                if ternary:
                    split_x(0)
                for g in range(G + 1):
                    if g < G:
                        for f in range(FT):
                            s = g * FT + f
                            dve.wait_ge(gated, s + 1)
                            if ternary and s >= 4:
                                dve.wait_ge(h_split, s - 3)
                            if not ternary and g >= 2 and f == 0:
                                dve.wait_ge(down_ready, KT * (g - 1))
                            up, out = banks[2 * (s % 3) + 1][:, :], h[:, s % 4, :] if ternary else h[:, g % 2, f, :]
                            if ternary:
                                dve.tensor_tensor(out, sg[:, s % 3, :], up, ALU.mult).then_inc(hidden, 1)
                            else:
                                dve.scalar_tensor_tensor(out=out, in0=up, scalar=us[:, f:f + 1],
                                                         in1=sg[:, s % 3, :], op0=ALU.mult,
                                                         op1=ALU.mult).then_inc(hidden, 1)
                            if ternary and f == 2 and g + 1 < G:
                                split_x(g + 1)
                    if g >= 1:
                        v = g - 1
                        for o in range(KT):
                            dve.wait_ge(down_ready, KT * v + o + 1)
                            if ternary:
                                dve.tensor_tensor(r[:, o, cols(v)], x[:, o, cols(v)], banks[6 + o][:, :],
                                                  ALU.add).then_inc(added, 1)
                            else:
                                dve.scalar_tensor_tensor(out=r[:, o, cols(v)], in0=banks[6 + o][:, :],
                                                         scalar=ds[:, o:o + 1], in1=x[:, o, cols(v)],
                                                         op0=ALU.mult, op1=ALU.add).then_inc(added, 1)


def projected_conv(nc, pairs, raw, steps, plain=()):
    S, T = len(steps), len(steps) + len(plain)
    with stage(nc, "product", "evacuated", "tapped", "ready", "chained") as (
            block, product, evacuated, tapped, ready, chained):
        @block.tensor
        def _(pe):
            for s, (w, cols, *_) in enumerate([*steps, *plain]):
                m = w.shape[2]
                if s >= 4:
                    pe.wait_ge(evacuated, s - 3)
                for j in range(L // W):
                    for c in range(KT):
                        mm = pe.matmul(pairs[s % 4][0:m, j * W:(j + 1) * W], w[:, c, :],
                                       cols[:, c, j * W:(j + 1) * W], start=c == 0, stop=c == KT - 1)
                mm.then_inc(product, 1)

        @block.scalar
        def _(act):
            def silu(s):
                act.wait_ge(tapped, s + 1)
                out = steps[s][4]
                act.activation(out, out, ACT.Silu).then_inc(ready, 1)

            for s, (w, cols, taps, bias, out) in enumerate(steps):
                m = w.shape[2]
                act.wait_ge(product, s + 1)
                if s >= 2:
                    act.wait_ge(tapped, s - 1)
                src = pairs[s % 4][0:m, :]
                act.activation(raw[0:m, s % 2, TAPS - 1:], src, ACT.Copy)
                if bias is None:
                    act.activation(out, src, ACT.Copy, scale=taps[:, TAPS - 1:TAPS]).then_inc(evacuated, 1)
                else:
                    act.activation(out, src, ACT.Identity, scale=taps[:, TAPS - 1:TAPS],
                                   bias=bias).then_inc(evacuated, 1)
                if s >= 1:
                    silu(s - 1)
            for s in range(S, T):
                act.wait_ge(product, s + 1)
                act.activation(plain[s - S][2], pairs[s % 4][:, :], ACT.Silu).then_inc(evacuated, 1)
                if s == S:
                    silu(S - 1)
            if S == T:
                silu(S - 1)

        @block.vector
        def _(dve):
            n = 0
            for s, (w, cols, taps, bias, out) in enumerate(steps):
                m = w.shape[2]
                dve.wait_ge(evacuated, s + 1)
                for j in range(TAPS - 1):
                    if j:
                        dve.wait_ge(chained, n)
                    ins = dve.scalar_tensor_tensor(out=out, in0=raw[0:m, s % 2, j:j + L],
                                                   scalar=taps[:, j:j + 1], in1=out,
                                                   op0=ALU.mult, op1=ALU.add)
                    if j < TAPS - 2:
                        ins.then_inc(chained, 1)
                        n += 1
                    else:
                        ins.then_inc(tapped, 1)


DT, UPTO_M, AFTER_M, ALL_M, LOGD_M = range(5)


def mamba_scalars(nc, k, banks, t, x):
    both = lambda ap: ap.rearrange("p (c b h) -> p c b h", b=B, h=MH)
    bias = t.per_head[:, 0, :].unsqueeze(1).unsqueeze(1).to_broadcast([P, NC, B, MH])
    rate = t.nega[:, :].unsqueeze(1).unsqueeze(1).to_broadcast([P, NC, B, MH])
    with stage(nc, "projected", "moved", "softened", "step", "sums_ready") as (
            block, projected, moved, softened, step, sums_ready):
        @block.tensor
        def _(pe):
            for c in range(NC):
                for b in range(B):
                    for kt in range(KT):
                        u = (c * B + b) * MH
                        mm = pe.matmul(banks[0][:, u:u + MH], x[:, kt, b * L + c * C:b * L + (c + 1) * C],
                                       t.w[:, kt, MIN - MH:], start=kt == 0, stop=kt == KT - 1)
            mm.then_inc(projected, 1)
            pe.wait_ge(step, 3)
            for j, m in enumerate((k.upto, k.after, k.ones)):
                mm = pe.matmul(banks[1 + j][:, 0:NC * B * MH], m[:, :],
                               t.u[:, 2, :, :, :].rearrange("p c b h -> p (c b h)"), start=True, stop=True)
            mm.then_inc(sums_ready, 1)

        @block.vector
        def _(dve):
            dve.wait_ge(projected, 1)
            dve.tensor_tensor(t.u[:, 0, :, :, :], both(banks[0][:, 0:NC * B * MH]), bias, ALU.add).then_inc(moved, 1)
            dve.wait_ge(moved, 1)
            dve.tensor_scalar(t.u[:, 2, :, :, :], t.u[:, 0, :, :, :], 0.0, None, ALU.max).then_inc(step, 1)
            dve.wait_ge(step, 1)
            dve.wait_ge(softened, 3)
            dve.tensor_tensor(t.all[:, :, :, DT, :], t.u[:, 2, :, :, :], t.u[:, 1, :, :, :], ALU.add).then_inc(step, 1)
            dve.wait_ge(step, 2)
            dve.tensor_tensor(t.u[:, 2, :, :, :], t.all[:, :, :, DT, :], rate, ALU.mult).then_inc(step, 1)
            dve.wait_ge(step, 3)
            dve.tensor_copy(t.all[:, :, :, LOGD_M, :], t.u[:, 2, :, :, :])

        @block.scalar
        def _(act):
            act.wait_ge(moved, 1)
            act.activation(t.u[:, 1, :, :, :], t.u[:, 0, :, :, :], ACT.Abs).then_inc(softened, 1)
            act.wait_ge(softened, 1)
            act.activation(t.u[:, 1, :, :, :], t.u[:, 1, :, :, :], ACT.Exp, scale=-1.0).then_inc(softened, 1)
            act.wait_ge(softened, 2)
            act.activation(t.u[:, 1, :, :, :], t.u[:, 1, :, :, :], ACT.Ln, bias=k.ones[:, 0:1]).then_inc(softened, 1)
            act.wait_ge(sums_ready, 1)
            for j in range(3):
                act.activation(t.all[:, :, :, UPTO_M + j, :], both(banks[1 + j][:, 0:NC * B * MH]), ACT.Exp)


def load_chunk(sp, t, x, i, staged):
    for b in range(B):
        cols = bass.ds(i * C + b * L, C)
        sp.dma_start(t.xc[:, b, :, :], x[:, :, cols]).then_inc(staged, 16)
        sp.dma_start(t.bx[:, b, 0:4, :], t.xbc[:, 0:4, cols]).then_inc(staged, 16)
        sp.dma_start(t.bx[0:DS, b, 4:6, :], t.xbc[0:DS, 4:6, cols]).then_inc(staged, 16)


def masked_decays(pool, k, t, i, copied):
    pool.tensor_copy(t.next[:, :, :], t.all[:, bass.ds(i, 1), :, LOGD_M, :].rearrange("p c b h -> p (c b) h")).then_inc(copied, 1)
    pool.wait_ge(copied, 1)
    for b in range(B):
        pool.tensor_tensor(t.gU[:, b, :, :], mid(k.upto[:, :], MH), last(t.next[:, b, :], C), ALU.mult)


def mamba_chunk(nc, k, banks, t, x, i, following):
    heads = lambda ap: ap.rearrange("p (h d) -> p h d", d=HD)
    span = (1, 5)
    gate_bank, turn_bank = (0, 7), (4, 3)
    with stage(nc, "current", "grams_ready", "spans_ready", "G_ready", "b_ready", "z_ready", "z_gated", "turned",
               "scaled_x", "x_used", "off_ready", "M_ready", "diag_ready", "state_ready", "y_step", "y_ready",
               "S_scaled", "squared", "std_ready", "inv_ready", "normed", "y_turned", "staged", "copied") as (
            block, current, grams_ready, spans_ready, G_ready, b_ready, z_ready, z_gated, turned,
            scaled_x, x_used, off_ready, M_ready, diag_ready, state_ready, y_step, y_ready,
            S_scaled, squared, std_ready, inv_ready, normed, y_turned, staged, copied):
        @block.sync
        def _(sp):
            if following is not None:
                sp.wait_ge(z_ready, B)
                sp.wait_ge(turned, B)
                sp.wait_ge(off_ready, B)
                load_chunk(sp, t, x, following, staged)
                sp.wait_ge(staged, 16 * 3 * B)

        @block.gpsimd
        def _(pool):
            if following is not None:
                pool.wait_ge(spans_ready, B)
                masked_decays(pool, k, t, following, copied)

        @block.tensor
        def _(pe):
            for b in range(B):
                pe.matmul(banks[3][:, b * C:(b + 1) * C], t.bx[0:DS, b, 4, :], t.bx[0:DS, b, 5, :],
                          start=True, stop=True)
            for b in range(B):
                at = B * C + b * DS
                mm = pe.transpose(banks[3][:, at:at + DS], t.bx[0:DS, b, 4, :], k.ident[0:DS, 0:DS])
            mm.then_inc(grams_ready, 1)
            for b in range(B):
                if b:
                    pe.wait_ge(x_used, b)
                for j in range(4):
                    mm = pe.transpose(banks[4][:, j * P:(j + 1) * P], t.bx[:, b, j, :], k.ident[:, :])
                mm.then_inc(turned, 1)
                for j in range(2):
                    pe.matmul(banks[span[b] + j][:, :], k.after[:, :],
                              t.gU[:, b, 4 * j:4 * j + 4, :].rearrange("p h l -> p (h l)"), start=True, stop=False)
                    mm = pe.matmul(banks[span[b] + j][:, :], k.identb[:, :], k.far[:, :], start=False, stop=True)
                mm.then_inc(spans_ready, 1)
            for b in range(B):
                for c in range(KT):
                    mm = pe.matmul(banks[gate_bank[b]][:, :], t.xc[:, b, c, :], t.w[:, c, 0:DI],
                                   start=c == 0, stop=c == KT - 1)
                mm.then_inc(z_ready, 1)
            for b in range(B):
                pe.wait_ge(G_ready, b + 1)
                pe.matmul(banks[span[b]][:, :], t.bx[0:DS, b, 5, :], t.S[:, b, :], start=True,
                          stop=True).then_inc(off_ready, 1)
            for b in range(B):
                pe.wait_ge(M_ready, b + 1)
                pe.wait_ge(x_used, b + 1)
                for h in range(MH):
                    mm = pe.matmul(banks[span[b] + 1][:, h * HD:(h + 1) * HD], t.M[:, b, h, :],
                                   t.xdt[:, b, h * HD:(h + 1) * HD], start=True, stop=True)
                mm.then_inc(diag_ready, 1)
                pe.wait_ge(b_ready, 1)
                pe.wait_ge(z_gated, b + 1)
                pe.matmul(banks[gate_bank[b]][0:DS, :], t.bt[:, b, :], t.xdd[:, b, :], start=True,
                          stop=True).then_inc(state_ready, 1)
            for b in range(B):
                pe.wait_ge(normed, b + 1)
                for j in range(4):
                    mm = pe.transpose(banks[turn_bank[b]][:, j * P:(j + 1) * P], t.yc[:, b, j * P:(j + 1) * P],
                                      k.ident[:, :])
                mm.then_inc(y_turned, 1)

        @block.scalar
        def _(act):
            for b in range(B):
                act.wait_ge(spans_ready, b + 1)
                act.activation(t.G[:, b, :, :].rearrange("p h l -> p (h l)"),
                               k.psum[:, span[b]:span[b] + 2, :].rearrange("p j l -> p (j l)"),
                               ACT.Exp).then_inc(G_ready, 1)
            act.wait_ge(grams_ready, 1)
            act.activation(t.bt[:, :, :].rearrange("p b n -> p (b n)"), banks[3][:, B * C:B * C + B * DS],
                           ACT.Copy).then_inc(b_ready, 1)
            for b in range(B):
                act.wait_ge(z_ready, b + 1)
                act.activation(t.sz[:, b, :], banks[gate_bank[b]][:, :], ACT.Silu).then_inc(z_gated, 1)
            for b in range(B):
                act.wait_ge(y_ready, b + 1)
                if b:
                    act.wait_ge(squared, b)
                act.activation(t.junk[:, :], t.yc[:, b, :], ACT.Square, accum_out=t.ss[:, b:b + 1]).then_inc(squared, 1)
            act.wait_ge(squared, B)
            act.activation(t.sd[:, 0, :], t.ss[:, :], ACT.Sqrt, scale=1.0 / DI, bias=k.eps5[:, :]).then_inc(std_ready, 1)

        @block.vector
        def _(dve):
            dve.tensor_copy(t.cur[:, :, :, :].rearrange("p b j h -> p (b j h)"),
                            t.all[:, bass.ds(i, 1), :, :, :].rearrange("p c b j h -> p (c b j h)")).then_inc(current, 1)
            dve.wait_ge(current, 1)
            for b in range(B):
                dve.wait_ge(turned, b + 1)
                xt = heads(banks[4][:, :])
                dve.tensor_tensor(heads(t.xdt[:, b, :]), xt, last(t.cur[:, b, DT, :], HD), ALU.mult).then_inc(scaled_x, 1)
                dve.tensor_tensor(heads(t.xd[:, b, :]), xt, last(t.per_head[:, 2, :], HD), ALU.mult)
                dve.wait_ge(scaled_x, b + 1)
                dve.tensor_tensor(heads(t.xdd[:, b, :]), heads(t.xdt[:, b, :]), last(t.cur[:, b, AFTER_M, :], HD),
                                  ALU.mult).then_inc(x_used, 1)
            dve.wait_ge(b_ready, 1)
            for b in range(B):
                dve.wait_ge(G_ready, b + 1)
                dve.tensor_tensor(t.M[:, b, :, :], t.G[:, b, :, :], mid(banks[3][:, b * C:(b + 1) * C], MH),
                                  ALU.mult).then_inc(M_ready, 1)
            for b in range(B):
                dve.wait_ge(off_ready, b + 1)
                dve.tensor_tensor(heads(t.yc[:, b, :]), heads(banks[span[b]][:, :]), last(t.cur[:, b, UPTO_M, :], HD),
                                  ALU.mult).then_inc(y_step, 1)
            for b in range(B):
                dve.wait_ge(y_step, b + 1)
                dve.wait_ge(x_used, b + 1)
                dve.tensor_tensor(t.yc[:, b, :], t.yc[:, b, :], t.xd[:, b, :], ALU.add).then_inc(y_step, 1)
            for b in range(B):
                dve.wait_ge(y_step, B + b + 1)
                dve.wait_ge(diag_ready, b + 1)
                dve.tensor_tensor(t.yc[:, b, :], t.yc[:, b, :], banks[span[b] + 1][:, :], ALU.add).then_inc(y_step, 1)
            for b in range(B):
                dve.wait_ge(y_step, 2 * B + b + 1)
                dve.wait_ge(z_gated, b + 1)
                dve.tensor_tensor(t.yc[:, b, :], t.yc[:, b, :], t.sz[:, b, :], ALU.mult).then_inc(y_ready, 1)
            for b in range(B):
                dve.tensor_tensor(heads(t.S[:, b, :]), heads(t.S[:, b, :]), last(t.cur[0:DS, b, ALL_M, :], HD),
                                  ALU.mult).then_inc(S_scaled, 1)
            for b in range(B):
                dve.wait_ge(S_scaled, b + 1)
                dve.wait_ge(state_ready, b + 1)
                dve.tensor_tensor(t.S[:, b, :], t.S[:, b, :], banks[gate_bank[b]][0:DS, :], ALU.add)
            dve.wait_ge(std_ready, 1)
            dve.reciprocal(t.sd[:, 1, :], t.sd[:, 0, :]).then_inc(inv_ready, 1)
            dve.wait_ge(inv_ready, 1)
            for b in range(B):
                dve.tensor_scalar(t.yc[:, b, :], t.yc[:, b, :], t.sd[:, 1, b:b + 1], None, ALU.mult).then_inc(normed, 1)
            for b in range(B):
                dve.wait_ge(y_turned, b + 1)
                dve.tensor_tensor(t.y[:, :, bass.ds(i * C + b * L, C)],
                                  banks[turn_bank[b]][:, :].rearrange("p (j l) -> p j l", l=C),
                                  last(t.nw[:, :], C), ALU.mult)


def mamba(nc, k, banks, pairs, x, r, a):
    with ExitStack() as ctx:
        sb = lambda n, s: ctx.enter_context(nc.sbuf_tensor(n, s, F32))
        w = sb("m_w", [P, KT, MIN])
        wo = sb("m_wo", [P, DI // P, D])
        taps = sb("m_taps", [P, 6, TAPS])
        cb = sb("m_cb", [P, 6])
        per_head = sb("m_heads", [P, 3, MH])
        nw = sb("m_nw", [P, DI // P])
        raw = sb("m_raw", [P, 2, TAPS - 1 + L])
        xbc = sb("m_xbc", [P, 6, N])
        y = sb("m_y", [P, DI // P, N])
        nega = sb("m_nega", [P, MH])
        S = sb("m_S", [DS, B, DI])
        with stage(nc, "loaded", "decayed") as (block, loaded, decayed):
            @block.sync
            def _(sp):
                sp.dma_start(w[:, :, :], a.in_proj.rearrange("(k p) f -> p k f", p=P)).then_inc(loaded, 16)
                sp.dma_start(wo[:, :, :], a.out_proj.rearrange("(k p) f -> p k f", p=P)).then_inc(loaded, 16)
                sp.dma_start(taps[:, 0:4, :], a.conv_w[0:DI, :].rearrange("(k p) j -> p k j", p=P)).then_inc(loaded, 16)
                sp.dma_start(taps[0:DS, 4:6, :], a.conv_w[DI:, :].rearrange("(k p) j -> p k j", p=DS)).then_inc(loaded, 16)
                sp.dma_start(cb[:, 0:4], a.conv_b[:, 0:4]).then_inc(loaded, 16)
                sp.dma_start(cb[0:DS, 4:6], a.conv_b[0:DS, 4:6]).then_inc(loaded, 16)
                sp.dma_start(per_head[:, :, :], a.mamba_heads).then_inc(loaded, 16)
                sp.dma_start(nw[:, :], a.mamba_norm).then_inc(loaded, 16)
                sp.wait_ge(loaded, 16 * 8)

            @block.vector
            def _(dve):
                dve.memset(raw[:, :, 0:TAPS - 1], 0.0)
                dve.memset(S[:, :, :], 0.0)
                dve.wait_ge(decayed, 1)
                dve.tensor_scalar(nega[:, :], nega[:, :], -1.0, None, ALU.mult)

            @block.scalar
            def _(act):
                act.wait_ge(loaded, 16 * 8)
                act.activation(nega[:, :], per_head[:, 1, :], ACT.Exp).then_inc(decayed, 1)

        steps = []
        for t in range(6):
            m, at = (P, DI + P * t) if t < 4 else (DS, 2 * DI + DS * (t - 4))
            for b in range(B):
                steps.append((w[:, :, at:at + m], x[:, :, b * L:(b + 1) * L], taps[0:m, t, :],
                              cb[0:m, t:t + 1], xbc[0:m, t, b * L:(b + 1) * L]))
        projected_conv(nc, pairs, raw, steps)

        with ExitStack() as inner:
            sb = lambda n, s: inner.enter_context(nc.sbuf_tensor(n, s, F32))
            t = Names()
            t.w, t.per_head, t.nega, t.nw, t.xbc, t.y, t.S = w, per_head, nega, nw, xbc, y, S
            t.xc, t.bx = sb("m_xc", [P, B, KT, C]), sb("m_bx", [P, B, 6, C])
            t.all = sb("m_all", [P, NC, B, 5, MH])
            t.cur, t.next = sb("m_cur", [P, B, 5, MH]), sb("m_next", [P, B, MH])
            t.u = sb("m_u", [P, 3, NC, B, MH])
            t.gU, t.G, t.M = (sb(n, [P, B, MH, C]) for n in ("m_gU", "m_G", "m_M"))
            t.sz, t.xdt, t.xdd, t.xd, t.yc = (sb(n, [P, B, DI]) for n in ("m_sz", "m_xdt", "m_xdd", "m_xd", "m_yc"))
            t.bt = sb("m_bt", [P, B, DS])
            t.ss, t.sd, t.junk = sb("m_ss", [P, B]), sb("m_sd", [P, 2, B]), sb("m_junk", [P, DI])
            mamba_scalars(nc, k, banks, t, x)
            with stage(nc, "staged", "copied") as (block, staged, copied):
                @block.sync
                def _(sp):
                    load_chunk(sp, t, x, 0, staged)
                    sp.wait_ge(staged, 16 * 3 * B)

                @block.gpsimd
                def _(pool):
                    masked_decays(pool, k, t, 0, copied)
            with nc.Fori(0, NC - 1) as i:
                mamba_chunk(nc, k, banks, t, x, i, i + 1)
            mamba_chunk(nc, k, banks, t, x, NC - 1, None)

        with stage(nc, "out_ready", "added") as (block, out_ready, added):
            @block.tensor
            def _(pe):
                for s in range(N // W * KT):
                    g, o = divmod(s, KT)
                    if s >= 4:
                        pe.wait_ge(added, s - 3)
                    for c in range(DI // P):
                        mm = pe.matmul(banks[s % 4][:, :], wo[:, c, o * P:(o + 1) * P],
                                       y[:, c, g * W:(g + 1) * W], start=c == 0, stop=c == DI // P - 1)
                    mm.then_inc(out_ready, 1)

            @block.vector
            def _(dve):
                for s in range(N // W * KT):
                    g, o = divmod(s, KT)
                    dve.wait_ge(out_ready, s + 1)
                    dve.tensor_tensor(r[:, o, g * W:(g + 1) * W], x[:, o, g * W:(g + 1) * W],
                                      banks[s % 4][:, :], ALU.add).then_inc(added, 1)


def delta_scalars(nc, k, banks, t, a, ctx_sb):
    HH = 2 * HV
    with stage(nc, "projected", "moved", "softened", "soft_done", "log_ready", "sums_ready", "exps_ready",
               "beta_exp", "step") as (
            block, projected, moved, softened, soft_done, log_ready, sums_ready, exps_ready, beta_exp, step):
        @block.tensor
        def _(pe):
            for c in range(NC):
                for j in range(KT):
                    mm = pe.matmul(banks[0][:, c * HH:(c + 1) * HH], t.x[:, j, c * C:(c + 1) * C],
                                   t.wba[:, j, :], start=j == 0, stop=j == KT - 1)
            mm.then_inc(projected, 1)
            pe.wait_ge(log_ready, 1)
            for j, m in enumerate((k.upto, k.after, k.ones)):
                mm = pe.matmul(banks[1 + j][:, 0:NC * HV], m[:, :],
                               t.g[:, :, :].rearrange("p c h -> p (c h)"), start=True, stop=True)
            mm.then_inc(sums_ready, 1)

        @block.vector
        def _(dve):
            ba = banks[0][:, :].rearrange("p (c h) -> p c h", h=HH)
            dve.wait_ge(projected, 1)
            dve.tensor_copy(t.beta[:, :, :], ba[:, :, 0:HV])
            dve.tensor_tensor(t.u[:, 0, :, :], ba[:, :, HV:], mid(t.heads[:, 0, :], NC), ALU.add).then_inc(moved, 1)
            dve.wait_ge(moved, 1)
            dve.tensor_scalar(t.u[:, 2, :, :], t.u[:, 0, :, :], 0.0, None, ALU.max).then_inc(step, 1)
            dve.wait_ge(softened, 3)
            dve.wait_ge(step, 1)
            dve.tensor_tensor(t.u[:, 2, :, :], t.u[:, 2, :, :], t.u[:, 1, :, :], ALU.add).then_inc(step, 1)
            dve.wait_ge(step, 2)
            dve.tensor_tensor(t.g[:, :, :], t.u[:, 2, :, :], mid(t.nega[:, :], NC), ALU.mult).then_inc(log_ready, 1)
            dve.wait_ge(beta_exp, 1)
            dve.tensor_scalar(t.beta[:, :, :], t.beta[:, :, :], 1.0, None, ALU.add).then_inc(step, 1)
            dve.wait_ge(step, 3)
            dve.reciprocal(t.beta[:, :, :], t.beta[:, :, :])

        @block.scalar
        def _(act):
            act.wait_ge(moved, 1)
            act.activation(t.beta[:, :, :], t.beta[:, :, :], ACT.Exp, scale=-1.0).then_inc(beta_exp, 1)
            act.activation(t.u[:, 1, :, :], t.u[:, 0, :, :], ACT.Abs).then_inc(softened, 1)
            act.wait_ge(softened, 1)
            act.activation(t.u[:, 1, :, :], t.u[:, 1, :, :], ACT.Exp, scale=-1.0).then_inc(softened, 1)
            act.wait_ge(softened, 2)
            act.activation(t.u[:, 1, :, :], t.u[:, 1, :, :], ACT.Ln, bias=k.ones[:, 0:1]).then_inc(softened, 1)
            act.wait_ge(sums_ready, 1)
            for j, out in enumerate((t.upto_exp, t.after_exp, t.all_exp)):
                act.activation(out[:, :, :].rearrange("p c h -> p (c h)"), banks[1 + j][:, 0:NC * HV], ACT.Exp)


BETA, UPTO, AFTER, ALL = range(4)
units = lambda m: m[:, :, :, :].rearrange("p c r l -> p (c r) l")
flat = lambda m, g: units(m)[:, 4 * g:4 * g + 4, :].rearrange("p u l -> p (u l)")
cut = lambda m, c: m[:, c * C:(c + 1) * C]
GR = U // 4
row = lambda m, h: m[bass.ds(h, 1)]


def invert(nc, k, banks, t, a, h, following):
    with stage(nc, "product", "moved", "added", "loaded", "weights_loaded") as (
            block, product, moved, added, loaded, weights_loaded):
        plan = [(t.LT, t.T, t.Z, None), (t.Z, None, t.ZT, None), (t.Z, t.TT, t.TT, t.TT),
                (t.ZT, t.Z, t.Z2, None), (t.Z2, None, t.ZT2, None), (t.Z2, t.TT, t.TT, t.TT),
                (t.ZT2, t.Z2, t.Z4, None), (t.Z4, t.TT, t.TT, t.TT), (t.eK, t.TT, t.WT, None)]
        order = [(s, g) for s in range(len(plan)) for g in range(GR)]
        mine = {True: [n for n, (s, g) in enumerate(order) if plan[s][3] is not None],
                False: [n for n, (s, g) in enumerate(order) if plan[s][3] is None]}
        place = {n: (kind, i + 1) for kind, ns in mine.items() for i, n in enumerate(ns)}

        def done(eng, n):
            kind, count = place[n]
            eng.wait_ge(added if kind else moved, count)

        @block.sync
        def _(sp):
            sp.dma_start(t.q2[:, :], t.q[:, :]).then_inc(loaded, 16)
            sp.dma_start(t.wo[:, :, :], row(a.w_out, h).rearrange("o p k f -> p (o k) f")).then_inc(weights_loaded, 16)
            if following is not None:
                load_weights(sp, t, a, following, loaded)
            sp.wait_ge(loaded, 16 + (32 if following is not None else 0))

        @block.tensor
        def _(pe):
            for n, (s, g) in enumerate(order):
                left, right, out, _ = plan[s]
                if n >= 8:
                    done(pe, n - 8)
                for m in (left, right):
                    written = [j for j in range(s) if plan[j][2] is m]
                    if written:
                        done(pe, written[-1] * GR + g)
                for u in range(4):
                    dst, lhs = banks[n % 8][:, u * C:(u + 1) * C], units(left)[:, 4 * g + u, :]
                    if right is None:
                        mm = pe.transpose(dst, lhs, t.ident[:, :])
                    else:
                        mm = pe.matmul(dst, lhs, units(right)[:, 4 * g + u, :], start=True, stop=True)
                mm.then_inc(product, 1)

        @block.scalar
        def _(act):
            for n in mine[False]:
                s, g = order[n]
                act.wait_ge(product, n + 1)
                act.activation(flat(plan[s][2], g), banks[n % 8][:, :], ACT.Copy).then_inc(moved, 1)

        @block.vector
        def _(dve):
            for n in mine[True]:
                s, g = order[n]
                dve.wait_ge(product, n + 1)
                if s > 2:
                    done(dve, [j for j in range(s) if plan[j][2] is t.TT][-1] * GR + g)
                dve.tensor_tensor(flat(plan[s][2], g), banks[n % 8][:, :], flat(plan[s][3], g),
                                  ALU.add).then_inc(added, 1)
            dve.wait_ge(weights_loaded, 16)
            wo = t.wo[:, :, :].rearrange("p r d -> p (r d)")
            dve.tensor_tensor(wo, wo, t.nw[:, :].to_broadcast([P, R * D]), ALU.mult)


def load_weights(sp, t, a, h, loaded):
    sp.dma_start(t.w[:, :, :], row(a.w_heads, h).rearrange("o p (k f) -> p (o k) f", k=KT)).then_inc(loaded, 16)
    sp.dma_start(t.taps[:, :, :], row(a.w_taps, h).rearrange("o p k f -> p (o k) f")).then_inc(loaded, 16)


def evacuate(act, t, s, src, out):
    act.activation(t.raw[:, s % 2, TAPS - 1:], src, ACT.Copy)
    return act.activation(out, src, ACT.Copy, scale=t.taps[:, s, TAPS - 1:TAPS])


def tap(dve, t, s, j, out):
    return dve.scalar_tensor_tensor(out=out, in0=t.raw[:, s % 2, j:j + L], scalar=t.taps[:, s, j:j + 1],
                                    in1=out, op0=ALU.mult, op1=ALU.add)


def scan_and_conv(nc, k, banks, t, h, scan, conv):
    pair = lambda bank: bank[:, 0:R * P]
    grouped = lambda ap: ap.rearrange("p (r l) -> p r l", r=R)
    with stage(nc, "cleared", "new_values", "values_moved", "off_ready", "off_moved", "state_add",
               "state_scaled", "state_ready", "diag_ready", "summed", "gated", "squared",
               "product", "evacuated", "chained", "tapped", "silu_done", "squares_ready", "norms_ready",
               "logd_ready") as (
            block, cleared, new_values, values_moved, off_ready, off_moved, state_add,
            state_scaled, state_ready, diag_ready, summed, gated, squared,
            product, evacuated, chained, tapped, silu_done, squares_ready, norms_ready, logd_ready):
        outs = (t.q[:, :], t.key[:, :], t.v[:, 0, :])
        slot = (1, 0)
        conv_pair = lambda s: t.pairs[2 + s % 2]

        @block.gpsimd
        def _(pool):
            if conv:
                pool.tensor_copy(t.logd[:, 0, :, :], t.g[:, :, bass.ds(R * h, R)]).then_inc(logd_ready, 1)
                pool.wait_ge(logd_ready, 1)
                pool.tensor_copy(t.logd_high[:, :, :], t.logd[:, 0, :, :]).then_inc(logd_ready, 1)
                pool.wait_ge(logd_ready, 2)
                high = t.logd_high[:, :, :].bitcast(F32)
                pool.tensor_tensor(t.logd[:, 1, :, :], t.logd[:, 0, :, :], high, ALU.subtract).then_inc(logd_ready, 1)
                pool.wait_ge(logd_ready, 3)
                for c in range(NC):
                    for n, part in enumerate((high, t.logd[:, 1, :, :])):
                        for r in range(R):
                            pool.tensor_scalar(t.gU[:, n, c, r, :], k.upto[:, :], part[:, c, r:r + 1], 1.0,
                                               ALU.mult, ALU.mult)

        @block.tensor
        def _(pe):
            def quarter(i):
                s, j, kt = i // 4, i // 2 % 2, i % 2
                if i == 8:
                    pe.wait_ge(evacuated, 1)
                mm = pe.matmul(conv_pair(s)[:, j * W:(j + 1) * W], t.w[:, kt, s * P:(s + 1) * P],
                               t.x[:, kt, j * W:(j + 1) * W], start=kt == 0, stop=kt == KT - 1)
                if i % 4 == 3:
                    mm.then_inc(product, 1)

            def norms(s):
                pe.wait_ge(evacuated, 2)
                pe.wait_ge(squares_ready, 2 - s)
                for c in range(NC):
                    at = slot[s] * NC + c
                    mm = pe.matmul(banks[6][:, at:at + 1], cut(t.sq[:, slot[s], :], c), k.ones[:, 0:1],
                                   start=True, stop=True)
                mm.then_inc(norms_ready, 1)

            for c in range(NC):
                if scan:
                    out = [banks[0][:, r * P:(r + 1) * P] for r in range(R)]
                    if c:
                        pe.wait_ge(values_moved, c)
                    for r in range(R):
                        pe.matmul(out[r], t.TT[:, c, r, :], t.V[:, c, r, :], start=r == 0, stop=False)
                    if c == 0:
                        pe.wait_ge(cleared, 1)
                    else:
                        pe.wait_ge(state_ready, c)
                    for r in range(R):
                        mm = pe.matmul(out[r], t.WT[:, c, r, :], t.S[:, r, :], start=False, stop=r == R - 1)
                    mm.then_inc(new_values, 1)
                    if c:
                        pe.wait_ge(off_moved, c)
                    pe.matmul(pair(banks[1]), cut(t.q2, c), t.S[:, :, :].rearrange("p r l -> p (r l)"),
                              start=True, stop=True).then_inc(off_ready, 1)
                if conv and c < 4:
                    quarter(3 * c)
                if scan:
                    pe.wait_ge(values_moved, c + 1)
                    for r in range(R):
                        mm = pe.matmul(banks[2][:, r * P:(r + 1) * P], t.Kd[:, c, r, :], t.Un[:, r, :],
                                       start=True, stop=True)
                    mm.then_inc(state_add, 1)
                    if c:
                        pe.wait_ge(gated, c)
                    for r in range(R):
                        pe.matmul(banks[3][:, r * P:(r + 1) * P], t.PT[:, c, r, :], t.Un[:, r, :],
                                  start=True, stop=True)
                    for r in range(R):
                        mm = pe.transpose(banks[3][:, (R + r) * P:(R + r + 1) * P], cut(t.z[:, r, :], c),
                                          t.ident[:, :])
                    mm.then_inc(diag_ready, 1)
                if conv and c < 4:
                    quarter(3 * c + 1)
                    quarter(3 * c + 2)
                if conv and c in (6, 7):
                    norms(7 - c)

        @block.scalar
        def _(act):
            def square(c):
                act.wait_ge(gated, c + 1)
                if c:
                    act.wait_ge(squared, c)
                for r in range(R):
                    ins = act.activation(t.junk[:, r, :], t.y[:, c, r, :], ACT.Square,
                                         accum_out=t.ss[:, c * R + r:c * R + r + 1])
                ins.then_inc(squared, 1)

            def silu(s):
                act.wait_ge(tapped, s + 1)
                act.activation(outs[s], outs[s], ACT.Silu).then_inc(silu_done, 1)

            def norm_squares(s):
                act.wait_ge(silu_done, s + 1)
                act.activation(t.sq[:, slot[s], :], outs[s], ACT.Square).then_inc(squares_ready, 1)

            for c in range(NC):
                if scan:
                    act.wait_ge(new_values, c + 1)
                    if c:
                        act.wait_ge(diag_ready, c)
                    act.activation(t.Un[:, :, :].rearrange("p r l -> p (r l)"), pair(banks[0]),
                                   ACT.Copy).then_inc(values_moved, 1)
                    act.wait_ge(off_ready, c + 1)
                    if c:
                        act.wait_ge(summed, c)
                    for r in range(R):
                        ins = act.activation(t.off[:, r, :], banks[1][:, r * P:(r + 1) * P], ACT.Copy,
                                             scale=t.mine[:, UPTO, c, r:r + 1])
                    ins.then_inc(off_moved, 1)
                if conv and c in (3, 5, 7):
                    silu(c // 2 - 1)
                if conv and c in (5, 6):
                    norm_squares(6 - c)
                if conv and c in (1, 2, 4):
                    s = (1, 2, 4).index(c)
                    act.wait_ge(product, s + 1)
                    evacuate(act, t, s, conv_pair(s), outs[s]).then_inc(evacuated, 1)
                if scan and c >= 1:
                    square(c - 1)
            if scan:
                square(NC - 1)

        @block.vector
        def _(dve):
            n = 0
            taps_at = ((), ((0, 0),), ((0, 1), (0, 2)), ((1, 0), (1, 1)), ((1, 2),), ((2, 0),), ((2, 1), (2, 2)), ())
            if scan:
                dve.memset(t.S[:, :, :], 0.0).then_inc(cleared, 1)
                dve.wait_ge(cleared, 1)
            for c in range(NC):
                if scan:
                    dve.wait_ge(off_ready, c + 1)
                    dve.wait_ge(new_values, c + 1)
                    if c:
                        dve.wait_ge(state_ready, c)
                    dve.tensor_tensor(t.S[:, :, :], t.S[:, :, :], last(t.mine[:, ALL, c, :], P),
                                      ALU.mult).then_inc(state_scaled, 1)
                    dve.wait_ge(state_scaled, c + 1)
                    dve.wait_ge(state_add, c + 1)
                    dve.tensor_tensor(t.S[:, :, :], t.S[:, :, :], grouped(pair(banks[2])), ALU.add).then_inc(state_ready, 1)
                    dve.wait_ge(diag_ready, c + 1)
                    dve.wait_ge(off_moved, c + 1)
                    dve.tensor_tensor(t.y[:, c, :, :], t.off[:, :, :], grouped(pair(banks[3])), ALU.add).then_inc(summed, 1)
                    dve.wait_ge(summed, c + 1)
                    dve.scalar_tensor_tensor(out=t.y[:, c, :, :].rearrange("p r l -> p (r l)"),
                                             in0=t.y[:, c, :, :].rearrange("p r l -> p (r l)"),
                                             scalar=t.inv[:, 1, c:c + 1], in1=banks[3][:, R * P:2 * R * P],
                                             op0=ALU.mult, op1=ALU.mult).then_inc(gated, 1)
                if conv:
                    for s, j in taps_at[c]:
                        if j == 0:
                            dve.wait_ge(evacuated, s + 1)
                        else:
                            dve.wait_ge(chained, n)
                        ins = tap(dve, t, s, j, outs[s])
                        if j < TAPS - 2:
                            ins.then_inc(chained, 1)
                            n += 1
                        else:
                            ins.then_inc(tapped, 1)
            if conv:
                dve.wait_ge(norms_ready, 2)
                dve.tensor_scalar(t.norm[:, :, :], banks[6][:, 0:2 * NC].rearrange("p (s c) -> p s c", s=2), 1e-6,
                                  None, ALU.add)


def front_and_tail(nc, k, banks, t, a, h, front, tail):
    with stage(nc, "mine_ready", "roots", "spans_ready", "G_ready", "grams", "E_ready", "P_ready", "TT_cleared",
               "chain", "blocks_out", "blocks_in", "inverse_cleared", "solve_step", "solved", "back_out", "back_in",
               "product", "evacuated", "chained", "tapped", "silu_done", "K_turned", "K_read", "V_turned", "V_read",
               "std_ready", "inv_ready", "normed", "y_turned", "y_moved", "z_ready", "z_moved", "out_ready",
               "added") as (
            block, mine_ready, roots, spans_ready, G_ready, grams, E_ready, P_ready, TT_cleared,
            chain, blocks_out, blocks_in, inverse_cleared, solve_step, solved, back_out, back_in,
            product, evacuated, chained, tapped, silu_done, K_turned, K_read, V_turned, V_read,
            std_ready, inv_ready, normed, y_turned, y_moved, z_ready, z_moved, out_ready, added):
        span_bank, out_bank = (0, 1, 6, 7), (4, 5, 2, 3)

        @block.gpsimd
        def _(pool):
            if front:
                pool.memset(t.TT[:, :, :, :], 0.0).then_inc(TT_cleared, 1)
                for c in range(NC):
                    pool.wait_ge(E_ready, c + 1)
                    pool.tensor_tensor(t.LT[:, c, :, :], t.E[:, c, :, :], mid(k.later_block[:, :], R), ALU.mult)
                for out, j in ((t.Kd, 2), (t.eK, 3)):
                    if j == 3:
                        pool.wait_ge(P_ready, 1)
                    for c in range(NC):
                        if j == 2 and c % 4 == 0:
                            pool.wait_ge(K_read, c // 4 + 1)
                        for r in range(R):
                            pool.tensor_scalar(out[:, c, r, :], cut(t.tokens, c), t.sc[:, j, c, r:r + 1], 1.0,
                                               ALU.mult, ALU.mult)

        @block.sync
        def _(sp):
            if front:
                sp.wait_ge(E_ready, NC)
                for r in range(NBL):
                    rows = slice(r * BL, (r + 1) * BL)
                    sp.dma_start(a.scratch[0, :, r, :, :].rearrange("u j i -> j u i"),
                                 units(t.E)[rows, :, rows]).then_inc(blocks_out, 16)
                sp.wait_ge(blocks_out, 16 * NBL)
                sp.dma_start(t.blk[:, :], a.scratch[0, :, :, :, :].rearrange("u r j i -> (u r) (j i)")).then_inc(blocks_in, 16)
                sp.wait_ge(solved, 1)
                sp.dma_start(a.scratch[1:3, :, :, :, :].rearrange("m u r j i -> (u r) m (j i)"),
                             t.inverse[:, :, :]).then_inc(back_out, 16)
                sp.wait_ge(back_out, 16)
                sp.wait_ge(TT_cleared, 1)
                for r in range(NBL):
                    rows = slice(r * BL, (r + 1) * BL)
                    sp.dma_start(t.inverses[rows, :, :, rows],
                                 a.scratch[1:3, :, r, :, :].rearrange("m u j i -> j m u i")).then_inc(back_in, 16)
                sp.wait_ge(back_in, 16 * NBL)

        @block.scalar
        def _(act):
            if front:
                for j in range(NC // 2):
                    act.wait_ge(spans_ready, j + 1)
                    act.activation(t.G[:, 2 * j:2 * j + 2, :, :].rearrange("p c r l -> p (c r l)"),
                                   banks[span_bank[j]][:, :], ACT.Exp).then_inc(G_ready, 1)
                act.activation(t.root[:, :, :], t.norm[:, :, :], ACT.Sqrt).then_inc(roots, 1)
                for half in range(2):
                    act.wait_ge(K_turned, half + 1)
                    act.activation(t.tokens[:, half * W:(half + 1) * W], banks[half][:, :], ACT.Copy).then_inc(K_read, 1)
            if tail:
                act.activation(t.std[:, :], t.ss[:, :], ACT.Sqrt, scale=1.0 / P, bias=k.eps6[:, :]).then_inc(std_ready, 1)
                act.wait_ge(inv_ready, 1)
                for g in range(GR):
                    for u in range(4 * g, 4 * g + 4):
                        ins = act.activation(units(t.y)[:, u, :], units(t.y)[:, u, :], ACT.Copy,
                                             scale=t.rstd[:, u:u + 1])
                    ins.then_inc(normed, 1)
            if tail:
                for g in range(GR):
                    act.wait_ge(y_turned, g + 1)
                    act.activation(t.yT[:, :, 2 * g * C:2 * (g + 1) * C].rearrange("p r (c l) -> p c r l", l=C),
                                   banks[4 + g % 2][:, :].rearrange("p (c r l) -> p c r l", r=R, l=C),
                                   ACT.Copy).then_inc(y_moved, 1)
            if front:
                act.wait_ge(product, 1)
                evacuate(act, t, 3, t.pairs[1], t.v[:, 1, :]).then_inc(evacuated, 1)
                for s in range(R * L // W):
                    if s == 2:
                        act.wait_ge(tapped, 1)
                        act.activation(t.v[:, 1, :], t.v[:, 1, :], ACT.Silu).then_inc(silu_done, 1)
                    act.wait_ge(z_ready, s + 1)
                    r, j = divmod(s, L // W)
                    act.activation(t.z[:, r, j * W:(j + 1) * W], banks[6 + s % 2][:, :], ACT.Silu).then_inc(z_moved, 1)

        @block.tensor
        def _(pe):
            def span(j):
                bank = banks[span_bank[j]]
                for n in range(2):
                    pe.matmul(bank[:, :], k.after_r[:, :],
                              t.gU[:, n, 2 * j:2 * j + 2, :, :].rearrange("p c r l -> p (c r l)"),
                              start=n == 0, stop=False)
                pe.matmul(bank[:, :], k.identb[:, :], k.far[:, :], start=False, stop=True).then_inc(spans_ready, 1)

            def gram(half, bank, rhs):
                for c in range(half * 4, half * 4 + 4):
                    mm = pe.matmul(bank[:, c % 4 * C:(c % 4 + 1) * C], cut(t.key, c), cut(rhs, c), start=True, stop=True)
                mm.then_inc(grams, 1)

            def turn_keys(half):
                for c in range(4):
                    mm = pe.transpose(cut(banks[half], c), cut(t.key, 4 * half + c), k.ident[:, :])
                mm.then_inc(K_turned, 1)

            def v_part(i):
                j, kt = divmod(i, KT)
                mm = pe.matmul(t.pairs[1][:, j * W:(j + 1) * W], t.w[:, kt, 3 * P:4 * P],
                               t.x[:, kt, j * W:(j + 1) * W], start=kt == 0, stop=kt == KT - 1)
                if i == KT * L // W - 1:
                    mm.then_inc(product, 1)

            def z_part(s):
                r, j = divmod(s, L // W)
                if s >= 2:
                    pe.wait_ge(z_moved, s - 1)
                for kt in range(KT):
                    mm = pe.matmul(banks[6 + s % 2][:, :], t.w[:, kt, (4 + r) * P:(5 + r) * P],
                                   t.x[:, kt, j * W:(j + 1) * W], start=kt == 0, stop=kt == KT - 1)
                mm.then_inc(z_ready, 1)

            if front:
                span(0)
                gram(0, banks[2], t.key)
                span(1)
                gram(1, banks[3], t.key)
                span(2)
                span(3)
                gram(0, banks[4], t.q)
                gram(1, banks[5], t.q)
                pe.wait_ge(G_ready, NC // 2)
                turn_keys(0)
                turn_keys(1)
                z_part(0)
                pe.wait_ge(E_ready, NC)
                for i in range(KT * L // W):
                    v_part(i)
                z_part(1)
            if tail:
                if front:
                    pe.wait_ge(P_ready, 1)
                for g in range(GR):
                    pe.wait_ge(normed, g + 1)
                    if g >= 2:
                        pe.wait_ge(y_moved, g - 1)
                    for j in range(4):
                        mm = pe.transpose(banks[4 + g % 2][:, j * C:(j + 1) * C], units(t.y)[:, 4 * g + j, :],
                                          k.ident[:, :])
                    mm.then_inc(y_turned, 1)
            if tail:
                pe.wait_ge(y_moved, GR)
                for s in range(KT * L // W):
                    j, o = divmod(s, KT)
                    if front and s == 2:
                        pe.wait_ge(evacuated, 1)
                    for r in range(R):
                        mm = pe.matmul(banks[out_bank[s]][:, :], t.wo[:, r, o * P:(o + 1) * P],
                                       t.yT[:, r, j * W:(j + 1) * W], start=r == 0, stop=r == R - 1)
                    mm.then_inc(out_ready, 1)
            if front:
                z_part(2)
                pe.wait_ge(K_read, 2)
                pe.wait_ge(silu_done, 1)
                for m in range(NC // 2):
                    if m >= 2:
                        pe.wait_ge(V_read, m - 1)
                    for u in range(2 * R):
                        mm = pe.transpose(cut(banks[m % 2], u), cut(t.v[:, u % R, :], 2 * m + u // R), k.ident[:, :])
                    mm.then_inc(V_turned, 1)
                    if m == 1:
                        z_part(3)

        @block.vector
        def _(dve):
            n = 0

            def link(ins):
                nonlocal n
                n += 1
                ins.then_inc(chain, 1)
                dve.wait_ge(chain, n)

            if front:
                dve.reciprocal(t.inv[:, 0, :], t.norm[:, 0, :])
                for j, src in enumerate((t.beta, t.upto_exp, t.after_exp, t.all_exp)):
                    ins = dve.tensor_copy(t.mine[:, j, :, :], src[:, :, bass.ds(R * h, R)])
                ins.then_inc(mine_ready, 1)
                dve.wait_ge(mine_ready, 1)
                link(dve.tensor_tensor(t.sc[:, 0, :, :], t.mine[:, BETA, :, :], last(t.inv[:, 0, :], R), ALU.mult))
                dve.tensor_scalar(t.sc[:, 1, :, :], t.sc[:, 0, :, :], -1.0, None, ALU.mult)
                dve.tensor_tensor(t.sc[:, 2, :, :], t.sc[:, 0, :, :], t.mine[:, AFTER, :, :], ALU.mult)
                link(dve.tensor_scalar(t.sc[:, 3, :, :], t.mine[:, UPTO, :, :], -1.0, None, ALU.mult))
                for c in range(NC):
                    dve.wait_ge(grams, c // 4 + 1)
                    dve.wait_ge(G_ready, c // 2 + 1)
                    for r in range(R):
                        ins = dve.scalar_tensor_tensor(out=t.E[:, c, r, :], in0=cut(banks[2 + c // 4], c % 4),
                                                       scalar=t.sc[:, 1, c, r:r + 1], in1=t.G[:, c, r, :],
                                                       op0=ALU.mult, op1=ALU.mult)
                    ins.then_inc(E_ready, 1)
            if tail:
                dve.wait_ge(std_ready, 1)
                dve.reciprocal(t.rstd[:, :], t.std[:, :]).then_inc(inv_ready, 1)
            if front:
                for c in range(NC):
                    dve.wait_ge(grams, 3 + c // 4)
                    for r in range(R):
                        ins = dve.scalar_tensor_tensor(out=t.PT[:, c, r, :], in0=cut(banks[4 + c // 4], c % 4),
                                                       scalar=t.sc[:, 0, c, r:r + 1], in1=t.G[:, c, r, :],
                                                       op0=ALU.mult, op1=ALU.mult)
                ins.then_inc(P_ready, 1)
                dve.wait_ge(roots, 1)
                link(dve.reciprocal(t.inv[:, 1, :], t.root[:, 1, :]))
                dve.tensor_scalar(t.inv[:, 1, :], t.inv[:, 1, :], P ** -0.5, None, ALU.mult)
                solve(dve, t, inverse_cleared, blocks_in, solve_step, solved)
                dve.wait_ge(evacuated, 1)
                for j in range(TAPS - 1):
                    if j:
                        dve.wait_ge(chained, j)
                    tap(dve, t, 3, j, t.v[:, 1, :]).then_inc(chained if j < TAPS - 2 else tapped, 1)
            if tail:
                for s in range(KT * L // W):
                    j, o = divmod(s, KT)
                    dve.wait_ge(out_ready, s + 1)
                    cols = slice(j * W, (j + 1) * W)
                    dve.tensor_tensor(t.acc[:, o, cols], t.acc[:, o, cols], banks[out_bank[s]][:, :],
                                      ALU.add).then_inc(added, 1)
            if front:
                for c in range(NC):
                    dve.wait_ge(V_turned, c // 2 + 1)
                    at = c % 2 * R * C
                    ins = dve.tensor_scalar(t.V[:, c, :, :].rearrange("p r l -> p (r l)"),
                                            banks[c // 2 % 2][:, at:at + R * C], t.root[:, 0, c:c + 1], None, ALU.mult)
                    if c % 2:
                        ins.then_inc(V_read, 1)


def solve(dve, t, cleared, blocks_in, solve_step, solved):
    tt = t.inverse[:, 0, :].rearrange("p (k i) -> p k i", i=BL)
    ebt = t.blk[:, :].rearrange("p (j i) -> p j i", i=BL)
    dve.memset(t.inverse[:, 0, :], 0.0).then_inc(cleared, 1)
    dve.wait_ge(cleared, 1)
    dve.memset(t.inverse[:, 0, ::BL + 1], 1.0).then_inc(cleared, 1)
    dve.wait_ge(cleared, 2)
    dve.wait_ge(blocks_in, 16)
    n = 0
    for i in range(1, BL):
        prod = t.prod[:, 0:i * i].rearrange("p (k j) -> p k j", j=i)
        dve.tensor_tensor(prod, tt[:, 0:i, 0:i],
                          ebt[:, 0:i, i:i + 1].rearrange("p j o -> p (o j)").unsqueeze(1).to_broadcast([P, i, i]),
                          ALU.mult).then_inc(solve_step, 1)
        n += 1
        dve.wait_ge(solve_step, n)
        dve.tensor_reduce(tt[:, 0:i, i], prod, AX, ALU.add).then_inc(solve_step, 1)
        n += 1
        dve.wait_ge(solve_step, n)
    dve.tensor_copy(t.inverse[:, 1, :].rearrange("p (i k) -> p i k", k=BL),
                    tt.rearrange("p k i -> p i k")).then_inc(solved, 1)


def delta(nc, k, banks, pairs, x, a):
    t = Names()
    with ExitStack() as ctx:
        sb = lambda n, s: ctx.enter_context(nc.sbuf_tensor("d_" + n, s, F32))
        t.x, t.acc = sb("x", [P, KT, L]), sb("acc", [P, KT, L])
        t.wba, t.heads, t.nega, t.nw = sb("wba", [P, KT, 2 * HV]), sb("heads", [P, 2, HV]), sb("nega", [P, HV]), sb("nw", [P, 1])
        t.beta, t.g, t.upto_exp, t.after_exp, t.all_exp = (
            sb(n, [P, NC, HV]) for n in ("beta", "g", "upto", "after", "all"))
        t.u = sb("u", [P, 3, NC, HV])
        t.w, t.taps, t.wo = sb("w", [P, KT, 6 * P]), sb("taps", [P, 4, TAPS]), sb("wo", [P, R, D])
        t.raw = sb("raw", [P, 2, TAPS - 1 + L])
        t.q, t.q2, t.key = sb("q", [P, L]), sb("q2", [P, L]), sb("k", [P, L])
        t.pairs, t.ident = pairs, k.ident
        t.v, t.z = sb("v", [P, R, L]), sb("z", [P, R, L])
        t.mine, t.sc, t.logd = sb("mine", [P, 4, NC, R]), sb("sc", [P, 4, NC, R]), sb("logd", [P, 2, NC, R])
        t.gU = ctx.enter_context(nc.sbuf_tensor("d_gU", [P, 2, NC, R, C], F32R))
        t.logd_high = ctx.enter_context(nc.sbuf_tensor("d_logd_high", [P, NC, R], F32R))
        t.norm, t.inv, t.root = (sb(n, [P, 2, NC]) for n in ("norm", "inv", "root"))
        full = lambda n: sb(n, [P, NC, R, C])
        t.E, t.G, t.LT, t.PT = full("E"), full("G"), full("LT"), full("PT")
        t.inverses = sb("inverses", [P, 2, U, C])
        t.TT, t.T = (t.inverses[:, m, :, :].rearrange("p (c r) l -> p c r l", r=R) for m in range(2))
        t.Kd, t.V = full("Kd"), full("V")
        t.ZT, t.Z2, t.ZT2 = full("ZT"), full("Z2"), full("ZT2")
        t.Z, t.eK, t.Z4, t.WT = t.E, t.G, t.ZT, t.LT
        t.blk, t.inverse, t.prod = sb("blk", [P, BL * BL]), sb("inverse", [P, 2, BL * BL]), sb("prod", [P, BL * BL])
        t.S, t.Un, t.off, t.junk = (sb(n, [P, 2, P]) for n in ("S", "Un", "off", "junk"))
        t.ss, t.std, t.rstd = (sb(n, [P, U]) for n in ("ss", "std", "rstd"))
        t.sq = t.ZT[:, :, :, :].rearrange("p c r l -> p (c r l)").rearrange("p (s l) -> p s l", s=2)
        t.tokens = t.ZT[:, 0:NC // 2, :, :].rearrange("p c r l -> p (c r l)")
        t.y, t.yT = t.Z2, t.ZT2[:, :, :, :].rearrange("p c r l -> p (c r l)").rearrange("p (r l) -> p r l", r=R)
        assert U * NBL == P
        with stage(nc, "loaded", "decayed") as (block, loaded, decayed):
            @block.sync
            def _(sp):
                sp.dma_start(t.wba[:, :, :], a.w_ba.rearrange("(k p) f -> p k f", p=P)).then_inc(loaded, 16)
                sp.dma_start(t.heads[:, :, :], a.delta_heads).then_inc(loaded, 16)
                sp.dma_start(t.nw[:, :], a.delta_norm).then_inc(loaded, 16)
                sp.wait_ge(loaded, 48)

            @block.scalar
            def _(act):
                act.wait_ge(loaded, 48)
                act.activation(t.nega[:, :], t.heads[:, 1, :], ACT.Exp).then_inc(decayed, 1)

            @block.vector
            def _(dve):
                dve.memset(t.raw[:, :, 0:TAPS - 1], 0.0)
                dve.wait_ge(decayed, 1)
                dve.tensor_scalar(t.nega[:, :], t.nega[:, :], -1.0, None, ALU.mult)

            @block.gpsimd
            def _(pool):
                pool.memset(t.T[:, :, :, :], 0.0)
        with nc.Fori(0, B) as b:
            with stage(nc, "copied") as (block, copied):
                @block.vector
                def _(dve):
                    dve.tensor_copy(t.x[:, :, :], x[:, :, bass.ds(b * L, L)]).then_inc(copied, 1)
                    dve.wait_ge(copied, 1)
                    dve.tensor_copy(t.acc[:, :, :], t.x[:, :, :])
            delta_scalars(nc, k, banks, t, a, None)
            with stage(nc, "loaded") as (block, loaded):
                @block.sync
                def _(sp):
                    load_weights(sp, t, a, 0, loaded)
                    sp.wait_ge(loaded, 32)
            scan_and_conv(nc, k, banks, t, 0, scan=False, conv=True)
            front_and_tail(nc, k, banks, t, a, 0, front=True, tail=False)
            with nc.Fori(0, HK - 1) as h:
                invert(nc, k, banks, t, a, h, h + 1)
                scan_and_conv(nc, k, banks, t, h + 1, scan=True, conv=True)
                front_and_tail(nc, k, banks, t, a, h + 1, front=True, tail=True)
            invert(nc, k, banks, t, a, HK - 1, None)
            scan_and_conv(nc, k, banks, t, None, scan=True, conv=False)
            front_and_tail(nc, k, banks, t, a, None, front=False, tail=True)
            with stage(nc, "copied") as (block, copied):
                @block.vector
                def _(dve):
                    dve.tensor_copy(x[:, :, bass.ds(b * L, L)], t.acc[:, :, :])


def program(nc, a, parts="mfdg"):
    k = Names()
    with ExitStack() as ctx:
        sb = lambda n, s, dt=F32: ctx.enter_context(nc.sbuf_tensor(n, s, dt))
        k.ident, k.identb, k.ones, k.mean_of = sb("ident", [P, P]), sb("identb", [P, P], BF16), sb("ones", [P, P]), sb("mean_of", [P, P])
        k.upto, k.after, k.later_block = sb("upto", [P, P]), sb("after", [P, P]), sb("later_block", [P, P])
        k.after_r = sb("after_r", [P, P], F32R)
        k.far = sb("far", [P, 4 * P], BF16)
        k.block_of, k.block_after = sb("block_of", [NBL, P]), sb("block_after", [NBL, P])
        k.eps5, k.eps6 = sb("eps5", [P, 1]), sb("eps6", [P, 1])
        x = sb("x", [P, KT, N])
        k.psum = ctx.enter_context(nc.psum_tensor("psum", [P, 8, W], F32))
        banks = [k.psum[:, i, :] for i in range(8)]
        pairs = [k.psum[:, 2 * i:2 * i + 2, :].rearrange("p j l -> p (j l)") for i in range(4)]
        constants(nc, k, banks)
        with stage(nc, "loaded") as (block, loaded):
            @block.sync
            def _(sp):
                sp.dma_start(x[:, :, :], a.x.rearrange("(k p) t -> p k t", p=P)).then_inc(loaded, 16)
                sp.wait_ge(loaded, 16)
        if "m" in parts:
            with nc.sbuf_tensor("r", [P, KT, N], F32) as r:
                mamba(nc, k, banks, pairs, x, r, a)
                layernorm(nc, k, banks, r, x, "mamba")
        if "f" in parts:
            with nc.sbuf_tensor("r2", [P, KT, N], F32) as r:
                ffn(nc, k, banks, x, r, "net0", a.w2, a.w1, a.w3, True)
                layernorm(nc, k, banks, r, x, "net0")
        if "d" in parts:
            delta(nc, k, banks, pairs, x, a)
            layernorm(nc, k, banks, x, x, "delta")
        if "g" in parts:
            with nc.sbuf_tensor("r3", [P, KT, N], F32) as r:
                ffn(nc, k, banks, x, r, "net1", a.up_w, a.gate_w, a.down_w, False, (a.gate_s, a.up_s, a.down_s))
                layernorm(nc, k, banks, r, x, "net1")
        with stage(nc, "stored") as (block, stored):
            @block.sync
            def _(sp):
                sp.dma_start(a.out.rearrange("(k p) t -> p k t", p=P), x[:, :, :]).then_inc(stored, 16)
                sp.wait_ge(stored, 16)


def layout(i):
    t = lambda m: np.ascontiguousarray(np.asarray(m).T)
    g = {n: np.asarray(v) for n, v in i.items()}
    rows = lambda *v: np.ascontiguousarray(np.broadcast_to(np.stack(v), (P, len(v), len(v[0]))))
    qkv, wz = g["L1_attn_W_qkv"], g["L1_attn_W_z"]
    kd = HK * P
    heads = [np.concatenate([qkv[:, h * P:(h + 1) * P], qkv[:, kd + h * P:kd + (h + 1) * P],
                             qkv[:, 2 * kd + R * h * P:2 * kd + R * (h + 1) * P],
                             wz[:, R * h * P:R * (h + 1) * P]], 1) for h in range(HK)]
    cw = g["L1_attn_conv_weight"]
    taps = [np.concatenate([cw[h * P:(h + 1) * P], cw[kd + h * P:kd + (h + 1) * P],
                            cw[2 * kd + R * h * P:2 * kd + R * (h + 1) * P]]) for h in range(HK)]
    cols = lambda v, p=P: np.ascontiguousarray(np.resize(v, (-(-len(v) // p), p)).T)
    conv_b = g["L0_attn_conv_b"]
    return {
        "x": t(g["L0_attn_x"].reshape(N, D)),
        "in_proj": t(g["L0_attn_in_proj_w"]), "out_proj": t(g["L0_attn_out_proj_w"]),
        "conv_w": g["L0_attn_conv_w"], "conv_b": np.concatenate([cols(conv_b[:DI]), np.resize(cols(conv_b[DI:], DS), (P, 2))], 1),
        "mamba_heads": rows(g["L0_attn_dt_bias"], g["L0_attn_A_log"], g["L0_attn_D"]),
        "mamba_norm": cols(g["L0_attn_norm_w"]),
        "w1": t(g["L0_ffn_w1"]), "w2": t(g["L0_ffn_w2"]), "w3": t(g["L0_ffn_w3"]),
        "w_heads": np.stack([h.reshape(KT, P, 6 * P).transpose(1, 0, 2).reshape(P, -1) for h in heads]),
        "w_taps": np.stack([h.reshape(4, P, TAPS).transpose(1, 0, 2) for h in taps]),
        "w_out": np.ascontiguousarray(g["L1_attn_W_out"].reshape(HK, R, P, D).transpose(0, 2, 1, 3)),
        "w_ba": np.concatenate([g["L1_attn_W_b"], g["L1_attn_W_a"]], 1),
        "delta_heads": rows(g["L1_attn_dt_bias"], g["L1_attn_A_log"]), "delta_norm": cols(g["L1_attn_norm_w"]),
        "gate_w": t(g["L1_ffn_gate_w"]), "up_w": t(g["L1_ffn_up_w"]), "down_w": t(g["L1_ffn_down_w"]),
        "gate_s": cols(g["L1_ffn_gate_s"]), "up_s": cols(g["L1_ffn_up_s"]), "down_s": cols(g["L1_ffn_down_s"]),
    }


def build(nc, arrays, parts="mfdg"):
    a = Names()
    dram = lambda n: nc.dram_tensor(f"in_{n}", arrays[n].shape, F32, kind="ExternalInput").ap()
    a.x, a.in_proj, a.out_proj, a.conv_w = dram("x"), dram("in_proj"), dram("out_proj"), dram("conv_w")
    a.conv_b, a.mamba_heads, a.mamba_norm = dram("conv_b"), dram("mamba_heads"), dram("mamba_norm")
    a.w1, a.w2, a.w3 = dram("w1"), dram("w2"), dram("w3")
    a.w_heads, a.w_taps, a.w_out, a.w_ba = dram("w_heads"), dram("w_taps"), dram("w_out"), dram("w_ba")
    a.delta_heads, a.delta_norm = dram("delta_heads"), dram("delta_norm")
    a.gate_w, a.up_w, a.down_w, a.gate_s = dram("gate_w"), dram("up_w"), dram("down_w"), dram("gate_s")
    a.up_s, a.down_s = dram("up_s"), dram("down_s")
    a.scratch = nc.dram_tensor("scratch", (3, U, NBL, BL, BL), F32, kind="Internal").ap()
    a.out = nc.dram_tensor("out", (D, N), F32, kind="ExternalOutput").ap()
    program(nc, a, parts)


def kernel(**inputs):
    import concourse.bacc as bacc
    from concourse.bass_utils import run_bass_kernel_spmd

    arrays = {n: np.ascontiguousarray(v) for n, v in layout(inputs).items()}
    nc = bacc.Bacc("TRN2", target_bir_lowering=False, num_devices=1)
    build(nc, arrays)
    result = run_bass_kernel_spmd(nc, [{f"in_{n}": v for n, v in arrays.items()}], core_ids=[0])
    return np.ascontiguousarray(result.results[0]["out"].T).reshape(B, L, D)
```
